# Optimizing a Trainium2 kernel written in Bass

```python
import numpy as np
import jax
import jax.numpy as jnp

def _softmax(x, axis=-1):
    return jax.nn.softmax(x, axis=axis)

def _gelu(x):
    return jax.nn.gelu(x, approximate=True)

def _silu(x):
    return jax.nn.silu(x)

def _sigmoid(x):
    return jax.nn.sigmoid(x)

def _layernorm(x, axis=-1, eps=1e-05):
    m = jnp.mean(x, axis=axis, keepdims=True)
    v = jnp.var(x, axis=axis, keepdims=True)
    return (x - m) / jnp.sqrt(v + eps)

def _scatter_add(tgt, idx, src, axis=0):
    return tgt.at[idx].add(src)

def _segment_sum(src, seg, n):
    return jax.ops.segment_sum(src, seg, n)
kernel_name = 'mk_seq_preln_d1_jaxref_r8_2e1bd5'

def setup_inputs(seed: int=0):
    np.random.seed(seed)
    _w = jnp.asarray

    def _L0_attn_setup():
        import math
        import jax, jax.numpy as jnp
        import numpy as np
        H = 16
        EPS = 1e-06

        def _rmsnorm(x, w):
            xf = x.astype(jnp.float32)
            y = xf * jax.lax.rsqrt(jnp.mean(xf * xf, axis=-1, keepdims=True) + EPS)
            return (y * w).astype(x.dtype)
        key = jax.random.key(seed)
        ks = jax.random.split(key, 4)
        B, S, D = (4, 192, 256)
        return {'x': jax.random.normal(ks[0], (B, S, D), jnp.float32), 'w_qkv': jax.random.normal(ks[1], (D, 3 * D), jnp.float32) * (1.0 / math.sqrt(D)), 'b_qkv': jnp.zeros((3 * D,), jnp.float32), 'q_ln_w': jnp.ones((D,), jnp.float32), 'k_ln_w': jnp.ones((D,), jnp.float32), 'w_out': jax.random.normal(ks[2], (D, D), jnp.float32) * (1.0 / math.sqrt(D)), 'b_out': jnp.zeros((D,), jnp.float32)}
    _L0_attn_in = _L0_attn_setup()

    def _L0_ffn_setup():
        import jax, jax.numpy as jnp
        import numpy as np
        HIDDEN = 256
        INTER = 688
        LUT_SIZE = 16

        def _ghost_linear(x, idx, lut):
            w = lut[idx]
            return jnp.einsum('bsh,oh->bso', x, w)
        key = jax.random.key(seed)
        k_x, k_lut, k_g, k_u, k_d = jax.random.split(key, 5)
        x = jax.random.normal(k_x, (2, 512, HIDDEN), dtype=jnp.float32)
        lut = jax.random.normal(k_lut, (LUT_SIZE,), dtype=jnp.float32) * 0.02
        gate_idx = jax.random.randint(k_g, (INTER, HIDDEN), 0, LUT_SIZE, dtype=jnp.int32)
        up_idx = jax.random.randint(k_u, (INTER, HIDDEN), 0, LUT_SIZE, dtype=jnp.int32)
        down_idx = jax.random.randint(k_d, (HIDDEN, INTER), 0, LUT_SIZE, dtype=jnp.int32)
        return {'x': x, 'lut': lut, 'gate_idx': gate_idx, 'up_idx': up_idx, 'down_idx': down_idx}
    _L0_ffn_in = _L0_ffn_setup()
    _d = {'L0_attn_x': _L0_attn_in['x'], 'L0_attn_w_qkv': _L0_attn_in['w_qkv'], 'L0_attn_b_qkv': _L0_attn_in['b_qkv'], 'L0_attn_q_ln_w': _L0_attn_in['q_ln_w'], 'L0_attn_k_ln_w': _L0_attn_in['k_ln_w'], 'L0_attn_w_out': _L0_attn_in['w_out'], 'L0_attn_b_out': _L0_attn_in['b_out'], 'L0_ffn_lut': _L0_ffn_in['lut'], 'L0_ffn_gate_idx': _L0_ffn_in['gate_idx'], 'L0_ffn_up_idx': _L0_ffn_in['up_idx'], 'L0_ffn_down_idx': _L0_ffn_in['down_idx']}
    _x0 = _d['L0_attn_x']
    _d['L0_attn_x'] = jax.random.normal(jax.random.fold_in(jax.random.key(seed), 1), (4, 1024, 256), dtype=_x0.dtype)
    del _x0
    return _d

def reference(L0_attn_x, L0_attn_w_qkv, L0_attn_b_qkv, L0_attn_q_ln_w, L0_attn_k_ln_w, L0_attn_w_out, L0_attn_b_out, L0_ffn_lut, L0_ffn_gate_idx, L0_ffn_up_idx, L0_ffn_down_idx):

    def _L0_attn_ref(x, w_qkv, b_qkv, q_ln_w, k_ln_w, w_out, b_out):
        import math
        import jax, jax.numpy as jnp
        import numpy as np
        H = 16
        EPS = 1e-06

        def _rmsnorm(x, w):
            xf = x.astype(jnp.float32)
            y = xf * jax.lax.rsqrt(jnp.mean(xf * xf, axis=-1, keepdims=True) + EPS)
            return (y * w).astype(x.dtype)
        B, S, D = x.shape
        hd = D // H
        scale = 1.0 / math.sqrt(hd)
        qkv = x @ w_qkv + b_qkv
        q, k, v = jnp.split(qkv, 3, axis=-1)
        q = _rmsnorm(q, q_ln_w)
        k = _rmsnorm(k, k_ln_w)
        q = q.reshape(B, S, H, hd).transpose(0, 2, 1, 3)
        k = k.reshape(B, S, H, hd).transpose(0, 2, 1, 3)
        v = v.reshape(B, S, H, hd).transpose(0, 2, 1, 3)
        scores = jnp.einsum('bhqd,bhkd->bhqk', q, k) * scale
        min_val = jnp.finfo(scores.dtype).min
        causal = jnp.tril(jnp.ones((S, S), dtype=bool))
        scores = jnp.where(causal[None, None], scores, min_val)
        probs = jax.nn.softmax(scores, axis=-1)
        out = jnp.einsum('bhqk,bhkd->bhqd', probs, v)
        out = out.transpose(0, 2, 1, 3).reshape(B, S, D)
        return out @ w_out + b_out

    def _L0_ffn_ref(x, lut, gate_idx, up_idx, down_idx):
        import jax, jax.numpy as jnp
        import numpy as np
        HIDDEN = 256
        INTER = 688
        LUT_SIZE = 16

        def _ghost_linear(x, idx, lut):
            w = lut[idx]
            return jnp.einsum('bsh,oh->bso', x, w)
        gate = _ghost_linear(x, gate_idx, lut)
        up = _ghost_linear(x, up_idx, lut)
        h = jax.nn.silu(gate) * up
        return _ghost_linear(h, down_idx, lut)
    x = L0_attn_x
    x = x + _L0_attn_ref(_layernorm(x, axis=-1), L0_attn_w_qkv, L0_attn_b_qkv, L0_attn_q_ln_w, L0_attn_k_ln_w, L0_attn_w_out, L0_attn_b_out)
    x = x + _L0_ffn_ref(_layernorm(x, axis=-1), L0_ffn_lut, L0_ffn_gate_idx, L0_ffn_up_idx, L0_ffn_down_idx)
    return x

_drawn_inputs = setup_inputs


def setup_inputs(seed=0):
    import zlib

    import numpy as np

    out = dict(_drawn_inputs(seed))
    spreads = {'L0_attn_b_qkv': (0.0, 0.1),
     'L0_attn_q_ln_w': (1.0, 0.6),
     'L0_attn_k_ln_w': (1.0, 0.587),
     'L0_attn_b_out': (0.0, 0.1)}
    factors = {}
    for name, (base, spread) in spreads.items():
        noise = np.random.default_rng([zlib.crc32(name.encode()), seed]).standard_normal(out[name].shape)
        drawn = base * np.exp(spread * noise) if base else spread * noise
        out[name] = jnp.asarray(drawn.astype(out[name].dtype))
    for name, factor in factors.items():
        out[name] = (out[name] * factor).astype(out[name].dtype)
    return out
```

```python
import struct
from contextlib import ExitStack

import concourse.bass as bass
from concourse import mybir

F32 = mybir.dt.float32
F32R = mybir.dt.float32r
BF16 = mybir.dt.bfloat16
I32 = mybir.dt.int32
ALU = mybir.AluOpType
ACT = mybir.ActivationFunctionType
AX_X = mybir.AxisListType.X

P = 128
BANK = 512
MASKED = -1.0e30
LEAST = -3.0e38
TWO_ONES = struct.unpack("<f", struct.pack("<I", 0x3F803F80))[0]


class Tally:

    def __init__(self, eng):
        self.eng, self.seen = eng, {}

    def __call__(self, sem, by=1):
        name = sem.name
        self.seen[name] = (sem, self.seen.get(name, (sem, 0))[1] + by)
        return self.seen[name][1]

    def count(self, sem):
        return self.seen.get(sem.name, (sem, 0))[1]

    def settle(self):
        self.eng.drain()
        for sem, n in self.seen.values():
            self.eng.sem_inc(sem, -n)
        self.seen = {}


def layer_kernel(nc, x, w_qkv, b_qkv, q_ln_w, k_ln_w, w_out, b_out, lut, gate_idx, up_idx, down_idx, out):
    B, S, D = x.shape
    H = 16
    HD = D // H
    INTER = gate_idx.shape[0]
    NLUT = lut.shape[0]
    KD = D // P
    RT = S // P
    GH = 4
    NG = H // GH
    QC = 256
    NQC = S // QC
    NTERM = 6
    Q_PART = [0, 0, 0, 1, 1, 2]
    K_PART = [0, 1, 2, 0, 1, 0]
    KROWS = NTERM * HD
    SROWS = KROWS + 3
    OC = (INTER + P - 1) // P
    OCP = OC * P
    LAST = INTER - (OC - 1) * P
    WCOLS = 2 * KD * OCP + OC * D
    UP0, DOWN0 = KD * OCP, 2 * KD * OCP
    NCH = WCOLS // BANK
    LUTB = NCH // (B - 1)
    assert NCH % (B - 1) == 0 and RT == 8 and KD == 2 and D == 256
    CH = 512
    NCHUNK = B * S // CH
    TC = CH // P

    UNITS = [(qc, kt) for qc in range(NQC) for kt in range(2 * qc + 2)]
    NU = len(UNITS)
    CHUNK_END = {UNITS.index((qc, 2 * qc + 1)): qc for qc in range(NQC)}

    def is_diag(l):
        qc, kt = UNITS[l]
        return kt >= 2 * qc

    def width(l):
        qc, kt = UNITS[l]
        return P if kt == 2 * qc + 1 else QC

    FILLS = [
        [(0, 0, 128, 0, True), (2, 0, 384, 128, True)],
        [(3, 0, 512, 0, True)],
        [(4, 0, 512, 0, False)],
        [(5, 0, 512, 0, False)],
        [(6, 0, 512, 0, False)],
        [(7, 0, 512, 0, False)],
        [(4, 512, 128, 0, True), (6, 512, 384, 128, True)],
        [(7, 512, 512, 0, True)],
        [(1, 0, 256, 0, True), (5, 512, 256, 256, True)],
    ]
    NF = len(FILLS) * GH
    FILL_UNITS = 12
    PER = NF // FILL_UNITS

    ORDER = []
    for t in range(RT + 1):
        if t < RT:
            ORDER += [("X", t), ("QK", t)]
        if t:
            ORDER.append(("T", t - 1))
    STATS_UNIT = FILL_UNITS

    def place_jobs(nxt):
        jobs = {u: [] for u in range(NG * NU)}
        for t, u in enumerate([0, 0, 1, 2, 3, 5, 6, 7]):
            jobs[u].append(("V", t))
        taken = set()
        for g in range(NG):
            for l, qc in CHUNK_END.items():
                u = NU * g + l + 3
                if u < NG * NU:
                    jobs[u].append(("C", g, qc))
                    taken.add(u)
            if g < NG - 1 or nxt:
                jobs[NU * g + FILL_UNITS + 1].append(("N", (g + 1) % NG))
                taken.add(NU * g + FILL_UNITS + 1)
        if nxt:
            free = [u for u in range(STATS_UNIT + 3, 3 * NU - 6) if u not in taken]
            for u, job in zip(free, ORDER, strict=False):
                jobs[u].append(job)
            assert len(free) >= len(ORDER)
        g0 = (NG - 1) * NU
        for u, job in [(5, ("OT", 0)), (6, ("OP", 0)), (7, ("OP", 1)), (9, ("OT", 1)), (10, ("OP", 2)),
                       (11, ("OP", 3)), (15, ("OT", 2)), (16, ("OP", 4)), (17, ("OP", 5))]:
            jobs[g0 + u].append(job)
        return jobs

    TAIL = [("C", NG - 1, NQC - 1), ("OT", 3), ("OP", 6), ("OP", 7)]

    with ExitStack() as ctx:
        def sb(name, shape, dt=F32):
            return ctx.enter_context(nc.sbuf_tensor(name, shape, dt))

        def sem(name):
            return ctx.enter_context(nc.semaphore(name))

        ident = sb("ident", [P, P])
        identb = sb("identb", [P, P], BF16)
        causal = sb("causal", [P, BANK], BF16)
        wqkv = sb("wqkv", [P, KD, 3 * D])
        wout = sb("wout", [P, KD, D])
        lnw = sb("lnw", [P, 2 * D])
        bias = sb("bias", [3, 4 * D], BF16)
        ones3 = sb("ones3", [3, P], BF16)
        lut_sb = sb("lut_sb", [P, NLUT])
        xin = sb("xin", [P, RT, D])
        xn = sb("xn", [P, 2, D])
        xnT = sb("xnT", [P, KD, S])
        stats = sb("stats", [P, RT, 6])
        mv = sb("mv", [P, RT, 2])
        var = sb("var", [P, RT])
        rstd = sb("rstd", [P, RT])
        minus_half = sb("minus_half", [P, RT])
        ss = sb("ss", [P, 2, 2])
        sse = sb("sse", [P, 2, 2])
        rs = sb("rs", [P, 2, 2])
        probs = sb("probs", [P, 2, GH, QC])
        maxj = sb("maxj", [P, 2, BANK], BF16)
        mdiag = sb("mdiag", [P, GH * RT])
        mfull = sb("mfull", [P, GH * RT])
        mrow = sb("mrow", [P, GH * RT])
        mrest = sb("mrest", [P, 2, GH * RT])
        mcut = sb("mcut", [P, 3, GH * RT], BF16)
        mcutT = sb("mcutT", [P, P], BF16)
        oT = sb("oT", [P, 2, QC])
        rden = sb("rden", [P, 2, GH])
        attn = sb("attn", [P, RT, D])
        attnT = sb("attnT", [P, 2, KD, P])
        xres = sb("xres", [P, 2, D])
        x2t = sb("x2t", [P, 2, D])
        idxT = sb("idxT", [P, WCOLS], BF16)
        wlook = sb("wlook", [P, WCOLS])
        picked = sb("picked", [P, 3, BANK])
        tick = sb("tick", [P, 8])
        with ExitStack() as attention:
            def sba(name, shape, dt=F32):
                return attention.enter_context(nc.sbuf_tensor(name, shape, dt))

            sqj = sba("sqj", [P, 2, D], BF16)
            qkraw = sba("qkraw", [P, 2, 2 * D])
            qkn = sba("qkn", [P, 2 * D])
            parts = sba("parts", [P, 3, 4, S], BF16)
            rest = sba("rest", [P, 2, BANK])
            qs = [sba(f"qs{g}", [P, GH, S], BF16) for g in range(NG)]
            ks = [sba(f"ks{g}", [P, GH, S], BF16) for g in range(NG)]
            vaug = sba("vaug", [P, RT, H, 32])
        whi = sb("whi", [P, WCOLS], F32R)
        wlo = sb("wlo", [P, WCOLS], F32R)
        xTh = sb("xTh", [P, 2, KD, CH], F32R)
        xTl = sb("xTl", [P, 2, KD, CH], F32R)
        hhi = sb("hhi", [P, OC, CH], F32R)
        hlo = sb("hlo", [P, OC, CH], F32R)
        parts_dram = nc.dram_tensor("parts_scratch", (3, 4, P, S), BF16, kind="Internal").ap()
        x2_dram = nc.dram_tensor("x2_scratch", (B * S, D), F32, kind="Internal").ap()

        sc = ctx.enter_context(nc.psum_tensor("sc", [P, 2, GH, QC], F32))
        mx = ctx.enter_context(nc.psum_tensor("mx", [P, 2, BANK], F32))
        ov = ctx.enter_context(nc.psum_tensor("ov", [P, BANK], F32))
        ms = ctx.enter_context(nc.psum_tensor("ms", [P, BANK], F32))
        scf = sc[:].rearrange("p a h q -> p (a h q)")
        MISC = [ms[:, :]] + [scf[:, BANK * i:BANK * (i + 1)] for i in range(3)]

        bias_in, consts_in, weights_in, x_in = sem("bias_in"), sem("consts_in"), sem("weights_in"), sem("x_in")
        bias_cut_ready, bias_placed, made = sem("bias_cut_ready"), sem("bias_placed"), sem("made")
        vaug_made = sem("vaug_made")
        idx_in, idx_used = [sem("idx_in0"), sem("idx_in1")], sem("idx_used")
        idx_cast, idx_bank, idx_bank_free = sem("idx_cast"), sem("idx_bank"), sem("idx_bank_free")
        xin_used = sem("xin_used")
        xn_ready, xn_free = sem("xn_ready"), sem("xn_free")
        misc_free = [sem(f"misc_free{i}") for i in range(4)]
        misc_act, misc_dve = sem("misc_act"), sem("misc_dve")
        var_ready, rstd_ready = sem("var_ready"), sem("rstd_ready")
        ss_ready, rs_ready, qkn_ready = sem("ss_ready"), sem("rs_ready"), sem("qkn_ready")
        p1_ready, r1_ready, p2_ready, rest_free = sem("p1_ready"), sem("r1_ready"), sem("p2_ready"), sem("rest_free")
        parts_ready, parts_stored = sem("parts_ready"), sem("parts_stored")
        stack_ready = [sem(f"stack_ready{g}") for g in range(NG)]
        stack_free = sem("stack_free")
        fill_ready, fill_free = sem("fill_ready"), sem("fill_free")
        mcut_ready, mcutT_ready = sem("mcut_ready"), sem("mcutT_ready")
        shift_ready = sem("shift_ready")
        sc_ready = sem("sc_ready")
        exp_full, exp_diag, masked = sem("exp_full"), sem("exp_diag"), sem("masked")
        av_done, oT_ready = sem("av_done"), sem("oT_ready")
        xres_in = [sem("xres_in0"), sem("xres_in1")]
        x2_ready = sem("x2_ready")
        x2_stored = [sem("x2_stored0"), sem("x2_stored1")]
        picked_ready, picked_free, lut_done = sem("picked_ready"), sem("picked_free"), sem("lut_done")
        dve_self, pool_self = sem("dve_self"), sem("pool_self")
        f_x2_in = [sem("f_x2_in0"), sem("f_x2_in1")]
        f_x2_used = sem("f_x2_used")
        f_w_ready, f_w_hi = sem("f_w_ready"), sem("f_w_hi")
        stacks_read = sem("stacks_read")
        f_xn_ready = sem("f_xn_ready")
        f_tr_ready, f_xhi_ready, f_xT_ready = sem("f_tr_ready"), sem("f_xhi_ready"), sem("f_xT_ready")
        f_gu_ready, f_silu_ready, f_gu_free, f_h_ready = sem("f_gu_ready"), sem("f_silu_ready"), sem("f_gu_free"), sem("f_h_ready")
        f_y_ready, f_y_free, f_out_ready = sem("f_y_ready"), sem("f_y_free"), sem("f_out_ready")
        f_stored = [sem("f_stored0"), sem("f_stored1")]

        x_rows = x.rearrange("b (t p) d -> b p t d", p=P)
        x_flat = x.rearrange("b s d -> (b s) d")
        out_flat = out.rearrange("b s d -> (b s) d")

        x2f = xin[:, :, :].rearrange("p (c t) d -> p c t d", c=2)
        silu = probs[:, :, :, :].rearrange("p a h q -> p a (h q)")[:, :, 0:CH]
        hf = xnT[:, :, 0:CH]
        yt = x2t
        xnf = attn[:, 0:TC, :]
        idx_i = probs[:, :, :, :].rearrange("p a h q -> p a (h q)").bitcast(I32)
        bias_row = attn[0:3, 0:4, :].rearrange("p a d -> p (a d)")
        bias_rest = attn[0:3, 4:8, :].rearrange("p a d -> p (a d)")
        bias_cut = picked[0:3, :, :].bitcast(BF16)
        idx_bf = oT[:, :, :].rearrange("p a q -> p (a q)").bitcast(BF16)
        GB = [scf[:, 0:BANK], scf[:, BANK:2 * BANK]]
        UB = [scf[:, 2 * BANK:3 * BANK], scf[:, 3 * BANK:4 * BANK]]
        YB = [mx[:, 0, :], mx[:, 1, :]]
        TB = [ov[:, :], ms[:, :]]

        block = ctx.enter_context(nc.Block())

        @block.sync
        def _(sp):
            n = Tally(sp)
            sp.dma_start(bias_row[:, 0:3 * D], b_qkv.partition_broadcast(3)).then_inc(bias_in, 16)
            sp.dma_start(bias_row[:, 3 * D:], b_out.partition_broadcast(3)).then_inc(bias_in, 16)
            sp.dma_start(xin[:, :, :], x_rows[0]).then_inc(x_in, 16)
            sp.dma_start(wqkv[:, :, :], w_qkv.rearrange("(k p) n -> p k n", p=P)).then_inc(weights_in, 16)
            sp.wait_ge(bias_cut_ready, 1)
            for i in range(3):
                sp.dma_start(bias[i:i + 1, :], bias_cut[i:i + 1, i, :]).then_inc(bias_placed, 16)
            sp.dma_start(lnw[:, 0:D], q_ln_w.partition_broadcast(P)).then_inc(consts_in, 16)
            sp.dma_start(lnw[:, D:], k_ln_w.partition_broadcast(P)).then_inc(consts_in, 16)
            sp.dma_start(wout[:, :, :], w_out.rearrange("(k p) n -> p k n", p=P)).then_inc(weights_in, 16)
            sp.dma_start(lut_sb[:, :], lut.partition_broadcast(P)).then_inc(consts_in, 16)

            def parts_out():
                for half in range(2):
                    sp.wait_ge(parts_ready, n(parts_ready))
                    cols = slice(half * S // 2, (half + 1) * S // 2)
                    sp.dma_start(parts_dram[:, :, :, cols].rearrange("i a p s -> p i a s"),
                                 parts[:, :, :, cols]).then_inc(parts_stored, 16)
                sp.wait_ge(parts_stored, n(parts_stored, 32))

            def stack(g):
                p0 = (g % 2) * (GH * HD)
                for dst, half, terms in ((qs[g], g // 2, Q_PART), (ks[g], 2 + g // 2, K_PART)):
                    for j, part in enumerate(terms):
                        sp.dma_start(dst[HD * j:HD * (j + 1), :, :],
                                     parts_dram[part, half, p0:p0 + GH * HD, :].rearrange("(h d) s -> d h s", h=GH)
                                     ).then_inc(stack_ready[g], 16)

            def shift(g):
                sp.wait_ge(mcutT_ready, n(mcutT_ready))
                for i in range(3):
                    sp.dma_start(qs[g][KROWS + i:KROWS + i + 1, :, :].rearrange("p h (t n) -> p (h t) n", n=P),
                                 mcutT[32 * i:32 * (i + 1), :]).then_inc(shift_ready, 16)

            sp.sem_inc(stack_free, 1)
            parts_out()
            for g in range(NG - 1):
                stack(g)
            shift(0)

            def body(b, nxt):
                if nxt:
                    sp.wait_ge(xin_used, n(xin_used))
                    sp.dma_start(xin[:, :, :], x_rows[b + 1]).then_inc(x_in, 16)
                sp.wait_ge(stack_free, n(stack_free))
                stack(NG - 1)
                shift(1)
                shift(2)
                if nxt:
                    sp.wait_ge(stack_free, n(stack_free))
                    parts_out()
                    stack(0)
                shift(3)
                if nxt:
                    sp.wait_ge(stack_free, n(stack_free))
                    stack(1)
                    sp.wait_ge(stack_free, n(stack_free))
                    stack(2)
                else:
                    sp.wait_ge(stack_free, n(stack_free, NG - 1))
                r0 = b * S
                for t in range(2):
                    sp.dma_start(xres[:, t, :], x_flat[bass.ds(r0 + t * P, P), :]).then_inc(xres_in[t], 16)
                for t in range(RT):
                    if t == 4 and nxt:
                        shift(0)
                    sp.wait_ge(x2_ready, n(x2_ready))
                    sp.dma_start(x2_dram[bass.ds(r0 + t * P, P), :], x2t[:, t % 2, :]).then_inc(x2_stored[t % 2], 16)
                    if t + 2 < RT:
                        sp.dma_start(xres[:, t % 2, :],
                                     x_flat[bass.ds(r0 + (t + 2) * P, P), :]).then_inc(xres_in[t % 2], 16)
                n.settle()

            n.settle()
            with sp.Fori(0, B - 1) as b:
                body(b, True)
            body(B - 1, False)

            for c in range(2):
                sp.wait_ge(f_x2_used, n(f_x2_used))
                sp.dma_start(x2f[:, c], x2_dram[c * CH:(c + 1) * CH, :].rearrange("(t p) d -> p t d", p=P)
                             ).then_inc(f_x2_in[c], 16)
            n.settle()

            def ffn_pair(i, more):
                for c in range(2):
                    r0 = (2 * i + c) * CH
                    for t in range(TC):
                        sp.wait_ge(f_out_ready, n(f_out_ready))
                        sp.dma_start(out_flat[bass.ds(r0 + t * P, P), :], yt[:, t % 2, :]).then_inc(f_stored[t % 2], 16)
                    if more:
                        sp.wait_ge(f_x2_used, n(f_x2_used))
                        sp.dma_start(x2f[:, c], x2_dram[bass.ds(r0 + 2 * CH, CH), :].rearrange("(t p) d -> p t d", p=P)
                                     ).then_inc(f_x2_in[c], 16)
                n.settle()

            with sp.Fori(0, NCHUNK // 2 - 1) as i:
                ffn_pair(i, True)
            ffn_pair(NCHUNK // 2 - 1, False)

        @block.gpsimd
        def _(pool):
            n = Tally(pool)
            nc.gpsimd.memset(ident[:, :], 0.0).then_inc(pool_self, 1)
            pool.wait_ge(pool_self, 1)
            nc.gpsimd.affine_select(out=ident[:, :], in_=ident[:, :], compare_op=ALU.not_equal, fill=1.0, base=0,
                                    pattern=[[-1, P]], channel_multiplier=1).then_inc(pool_self, 1)
            pool.wait_ge(pool_self, 2)
            nc.gpsimd.tensor_copy(identb[:, :], ident[:, :])
            nc.gpsimd.memset(causal[:, :], 0.0).then_inc(pool_self, 1)
            pool.wait_ge(pool_self, 3)
            tri = causal[:, BANK - P:]
            nc.gpsimd.affine_select(out=tri, in_=tri, compare_op=ALU.is_ge, fill=MASKED, base=0,
                                    pattern=[[-1, P]], channel_multiplier=1)
            nc.gpsimd.memset(minus_half[:, :], -0.5)
            nc.gpsimd.memset(tick[:, :], 0.0)
            pool.drain().then_inc(made, 1)

            def last_part(t):
                pool.wait_ge(p2_ready, n(p2_ready))
                r = rest[:, t % 2, :].rearrange("p (a r) -> p a r", a=4)
                cols = slice(t * P, (t + 1) * P)
                nc.gpsimd.tensor_tensor(parts[:, 2, :, cols], r, parts[:, 1, :, cols],
                                        ALU.subtract).then_inc(rest_free, 1)
                if t % (RT // 2) == RT // 2 - 1:
                    pool.drain().then_inc(parts_ready, 1)

            def roots_of_rows(m):
                pool.wait_ge(var_ready, n(var_ready))
                nc.gpsimd.tensor_tensor(rstd[:, 0:m], var[:, 0:m], minus_half[:, 0:m], ALU.pow).then_inc(rstd_ready, 1)

            def roots_of_qk(t):
                pool.wait_ge(ss_ready, n(ss_ready))
                nc.gpsimd.tensor_scalar(sse[:, t % 2, :], ss[:, t % 2, :], D * 1e-6, None, ALU.add).then_inc(pool_self, 1)
                pool.wait_ge(pool_self, n(pool_self))
                nc.gpsimd.tensor_tensor(rs[:, t % 2, :], sse[:, t % 2, :], minus_half[:, 0:2],
                                        ALU.pow).then_inc(rs_ready, 1)

            pool.sem_inc(pool_self, -3)
            roots_of_rows(RT)
            for kind, t in ORDER:
                if kind == "QK":
                    roots_of_qk(t)
                elif kind == "T":
                    last_part(t)
            nc.gpsimd.memset(vaug[:, :, :, :].rearrange("p t h c -> p (t h c)"), 0.0).then_inc(pool_self, 1)
            pool.wait_ge(pool_self, n(pool_self))
            nc.gpsimd.memset(vaug[:, :, :, HD:HD + 1], 1.0).then_inc(vaug_made, 1)
            nc.gpsimd.memset(wlook[:, :], 0.0)
            n.settle()

            def body(b, nxt):
                jobs = place_jobs(nxt)
                step = 0
                for u in range(NG * NU):
                    l = u % NU
                    if is_diag(l):
                        pool.wait_ge(exp_diag, n(exp_diag))
                        p = probs[:, u % 2, :, 0:P]
                        nc.gpsimd.affine_select(out=p, in_=p, compare_op=ALU.is_ge, fill=0.0, base=0,
                                                pattern=[[0, GH], [1, P]], channel_multiplier=-1).then_inc(masked, 1)
                    for job in jobs[u - 1] if u else []:
                        if job[0] == "T":
                            last_part(job[1])
                        elif job[0] == "QK":
                            roots_of_qk(job[1])
                    if nxt and u == STATS_UNIT + 1:
                        roots_of_rows(RT)
                    if nxt and FILL_UNITS <= l < FILL_UNITS + 6:
                        for _ in range(2):
                            i = step % LUTB
                            pool.wait_ge(picked_ready, n(picked_ready))
                            w = wlook[:, bass.ds((b * LUTB + i) * BANK, BANK)]
                            nc.gpsimd.tensor_tensor(w, w, picked[:, step % 3, :], ALU.add).then_inc(picked_free, 1)
                            step += 1
                n.settle()

            with pool.Fori(0, B - 1) as b:
                body(b, True)
            body(B - 1, False)
            pool.drain().then_inc(lut_done, 1)
            roots_of_rows(TC)
            n.settle()
            with pool.Fori(0, NCHUNK // 2 - 1) as i:
                roots_of_rows(TC)
                roots_of_rows(TC)
                n.settle()
            roots_of_rows(TC)

        @block.scalar
        def _(act):
            n = Tally(act)

            def x_part(t):
                act.wait_ge(misc_act, n(misc_act))
                k = bank()
                nc.scalar.copy(xnT[:, :, t * P:(t + 1) * P],
                               MISC[k][:, 0:D].rearrange("p (k r) -> p k r", k=KD)).then_inc(misc_free[k], 1)

            def qk_part(t):
                act.wait_ge(misc_act, n(misc_act))
                k = bank()
                nc.scalar.copy(qkraw[:, t % 2, :], MISC[k])
                nc.scalar.activation(sqj[:, 0, :], MISC[k][:, 0:D], ACT.Square, accum_out=ss[:, t % 2, 0:1])
                nc.scalar.activation(sqj[:, 1, :], MISC[k][:, D:], ACT.Square,
                                     accum_out=ss[:, t % 2, 1:2]).then_inc(ss_ready, 1)
                nc.scalar.copy(tick[0:1, 5:6], tick[0:1, 4:5]).then_inc(misc_free[k], 1)

            def t_part(t):
                act.wait_ge(misc_act, n(misc_act))
                k = bank()
                nc.scalar.copy(parts[:, 0, :, t * P:(t + 1) * P],
                               MISC[k].rearrange("p (a r) -> p a r", a=4)).then_inc(p1_ready, 1)

            def second_part(t):
                act.wait_ge(r1_ready, n(r1_ready))
                nc.scalar.copy(parts[:, 1, :, t * P:(t + 1) * P],
                               rest[:, t % 2, :].rearrange("p (a r) -> p a r", a=4)).then_inc(p2_ready, 1)

            turn = [0]
            NB = 4

            def bank():
                k = turn[0] % NB
                turn[0] += 1
                return k

            def skip():
                turn[0] += 1

            IDX = [(src, oc * P, min(P, INTER - oc * P), D) for src in (gate_idx, up_idx) for oc in range(OC)]
            IDX += [(down_idx, hb * P, P, INTER) for hb in range(KD)]

            def load_indices(m):
                src, r0, rows, wide = IDX[m]
                if m >= 2:
                    act.wait_ge(idx_used, n(idx_used))
                act.dma_start(idx_i[0:rows, m % 2, 0:wide], src[r0:r0 + rows, :]).then_inc(idx_in[m % 2], 16)

            load_indices(0)
            load_indices(1)
            act.wait_ge(made, 1)
            for kind, t in ORDER:
                if kind == "X":
                    x_part(t)
                elif kind == "QK":
                    qk_part(t)
                else:
                    t_part(t)
                    second_part(t)
            for m in range(2, len(IDX)):
                load_indices(m)
            act.wait_ge(vaug_made, 1)
            n.settle()

            def body(b, nxt):
                nonlocal NB
                NB = 1
                jobs = place_jobs(nxt)

                def out_chunk(u):
                    act.wait_ge(av_done, u + 1)
                    c = u // NU * NQC + CHUNK_END[u % NU]
                    nc.scalar.copy(oT[:, c % 2, :], ov[:, 0:QC]).then_inc(oT_ready, 1)

                def job_part(job):
                    kind = job[0]
                    if kind == "V":
                        act.wait_ge(misc_act, n(misc_act))
                        nc.scalar.copy(vaug[:, job[1], :, 0:HD],
                                       ms[:, 0:D].rearrange("p (h c) -> p h c", h=H)).then_inc(misc_free[0], 1)
                    elif kind == "X":
                        x_part(job[1])
                    elif kind == "QK":
                        qk_part(job[1])
                    elif kind == "T":
                        t_part(job[1])
                    elif kind == "OT":
                        act.wait_ge(misc_act, n(misc_act))
                        nc.scalar.copy(attnT[:, :, :, :].rearrange("p t k r -> p (t k r)"),
                                       ms[:, :]).then_inc(misc_free[0], 1)

                for u in range(NG * NU):
                    l = u % NU
                    if u >= 2:
                        if (l - 2) % NU in CHUNK_END:
                            out_chunk(u - 2)
                        act.wait_ge(av_done, u - 1)
                    n(av_done)
                    act.wait_ge(sc_ready, n(sc_ready))
                    w = width(l)
                    s = sc[:, u % 2, :, 0:w]
                    p = probs[:, u % 2, :, 0:w]
                    nc.scalar.activation(p, s, ACT.Exp).then_inc(exp_diag if is_diag(l) else exp_full, 1)
                    for job in jobs[u - 1] if u else []:
                        if job[0] == "T":
                            second_part(job[1])
                    for job in jobs[u]:
                        job_part(job)
                out_chunk(NG * NU - 1)
                for job in TAIL:
                    job_part(job)
                n.settle()

            with act.Fori(0, B - 1) as b:
                body(b, True)
            body(B - 1, False)

            def x_high(c, p):
                act.wait_ge(f_tr_ready, n(f_tr_ready))
                nc.scalar.copy(xTh[:, c, :, 2 * p * P:2 * (p + 1) * P].rearrange("p k (t r) -> p t k r", t=2),
                               TB[p].rearrange("p (t k r) -> p t k r", t=2, k=KD)).then_inc(f_xhi_ready, 1)

            act.wait_ge(lut_done, 1)
            act.wait_ge(stacks_read, 1)
            nc.scalar.copy(whi[:, :], wlook[:, :]).then_inc(f_w_hi, 1)
            for p in range(2):
                x_high(0, p)
            n.settle()

            def ffn_pair(more):
                for c in range(2):
                    for oc in range(OC):
                        act.wait_ge(f_gu_ready, n(f_gu_ready))
                        nc.scalar.activation(silu[:, oc % 2, :], GB[oc % 2], ACT.Silu).then_inc(f_silu_ready, 1)
                        if oc in (2, 4) and (more or c == 0):
                            x_high(1 - c, oc // 2 - 1)
                n.settle()

            with act.Fori(0, NCHUNK // 2 - 1) as i:
                ffn_pair(True)
            ffn_pair(False)

        @block.vector
        def _(dve):
            n = Tally(dve)

            def own():
                nc.vector.engine_nop().then_inc(dve_self, 1)
                dve.wait_ge(dve_self, n(dve_self))

            def signal(s):
                nc.vector.engine_nop().then_inc(s, 1)

            nc.vector.memset(ones3[:, :], 1.0)
            dve.wait_ge(bias_in, 16 * 2)
            nc.vector.tensor_copy(bias_cut[:, 0, :], bias_row[:, :])
            own()
            nc.vector.tensor_tensor(bias_rest[:, :], bias_row[:, :], bias_cut[:, 0, :], ALU.subtract)
            own()
            nc.vector.tensor_copy(bias_cut[:, 1, :], bias_rest[:, :])
            own()
            nc.vector.tensor_tensor(bias_cut[:, 2, :], bias_rest[:, :], bias_cut[:, 1, :],
                                    ALU.subtract).then_inc(bias_cut_ready, 1)

            def row_stats(rows):
                for t, row in enumerate(rows):
                    nc.vector.bn_stats(stats[:, t, :], row)
                own()
                for t in range(len(rows)):
                    nc.vector.bn_aggr(mv[:, t, :], stats[:, t, :])
                own()
                nc.vector.tensor_scalar(var[:, 0:len(rows)], mv[:, 0:len(rows), 1], 1e-5, None, ALU.add).then_inc(var_ready, 1)

            def normed(to, row, t):
                return nc.vector.tensor_scalar(to, row, mv[:, t, 0:1], rstd[:, t:t + 1], ALU.subtract, ALU.mult)

            def batch_stats():
                dve.wait_ge(x_in, n(x_in, 16))
                row_stats([xin[:, t, :] for t in range(RT)])

            def norm_tile(t):
                if t == 0:
                    dve.wait_ge(rstd_ready, n(rstd_ready))
                dve.wait_ge(xn_free, n(xn_free))
                normed(xn[:, t % 2, :], xin[:, t, :], t).then_inc(xn_ready, 1)
                if t == RT - 1:
                    signal(xin_used)

            def qk_norm(t):
                dve.wait_ge(rs_ready, n(rs_ready))
                for i in range(2):
                    last = nc.vector.scalar_tensor_tensor(
                        out=qkn[:, i * D:(i + 1) * D], in0=qkraw[:, t % 2, i * D:(i + 1) * D],
                        scalar=rs[:, t % 2, i:i + 1], in1=lnw[:, i * D:(i + 1) * D], op0=ALU.mult, op1=ALU.mult)
                last.then_inc(qkn_ready, 1)

            def t_part(t):
                dve.wait_ge(rest_free, n(rest_free))
                dve.wait_ge(p1_ready, n(p1_ready))
                k = bank()
                nc.vector.tensor_tensor(rest[:, t % 2, :].rearrange("p (a r) -> p a r", a=4),
                                        MISC[k].rearrange("p (a r) -> p a r", a=4),
                                        parts[:, 0, :, t * P:(t + 1) * P], ALU.subtract).then_inc(misc_free[k], 1)
                signal(r1_ready)
                if t + 1 < RT:
                    qk_norm(t + 1)

            def fill_part(f):
                dve.wait_ge(fill_ready, n(fill_ready))
                h, pieces = f // len(FILLS), FILLS[f % len(FILLS)]
                for qt, k0, w, col, diag in pieces:
                    src = mx[:, f % 2, col:col + w]
                    at = slice(h * RT + qt, h * RT + qt + 1)
                    if diag:
                        last = nc.vector.tensor_tensor_reduce(
                            out=maxj[:, f % 2, col:col + w], in0=src, in1=causal[:, BANK - w:], scale=1.0, scalar=LEAST,
                            op0=ALU.add, op1=ALU.max, accum_out=mdiag[:, at])
                    else:
                        last = nc.vector.reduce_max(mfull[:, at], src, AX_X)
                last.then_inc(fill_free, 1)

            def cut_maxima():
                own()
                nc.vector.tensor_tensor(mrow[:, :], mdiag[:, :], mfull[:, :], ALU.max)
                own()
                nc.vector.tensor_scalar(mrest[:, 0, :], mrow[:, :], -1.0, None, ALU.mult)
                own()
                nc.vector.tensor_copy(mcut[:, 0, :], mrest[:, 0, :])
                own()
                nc.vector.tensor_tensor(mrest[:, 1, :], mrest[:, 0, :], mcut[:, 0, :], ALU.subtract)
                own()
                nc.vector.tensor_copy(mcut[:, 1, :], mrest[:, 1, :])
                own()
                nc.vector.tensor_tensor(mcut[:, 2, :], mrest[:, 1, :], mcut[:, 1, :],
                                        ALU.subtract).then_inc(mcut_ready, 1)

            def n_part():
                dve.wait_ge(misc_dve, n(misc_dve))
                k = bank()
                nc.vector.tensor_copy(mcutT[0:96, :], MISC[k][0:96, 0:P // 2].bitcast(BF16)).then_inc(misc_free[k], 1)
                signal(mcutT_ready)

            turn = [0]
            NB = 4

            def bank():
                k = turn[0] % NB
                turn[0] += 1
                return k

            dve.sem_inc(xn_free, 2)
            dve.sem_inc(rest_free, 2)
            batch_stats()
            norm_tile(0)
            norm_tile(1)
            dve.wait_ge(consts_in, 16 * 3)
            nc.vector.tensor_scalar(lnw[:, 0:D], lnw[:, 0:D], float(D ** 0.5) / float(HD ** 0.5), None, ALU.mult)
            nc.vector.tensor_scalar(lnw[:, D:], lnw[:, D:], float(D ** 0.5), None, ALU.mult)
            own()
            for kind, t in ORDER:
                if kind == "X" and 0 < t < RT - 1:
                    norm_tile(t + 1)
                if (kind, t) == ("QK", 0):
                    qk_norm(0)
                if kind == "T":
                    t_part(t)
                else:
                    turn[0] += 1
            n.settle()
            nc.vector.memset(mfull[:, :], LEAST)
            for g in range(NG):
                nc.vector.memset(ks[g][KROWS:SROWS, :, :].rearrange("p h s -> p (h s)").bitcast(F32), TWO_ONES)
            for c in [k * OCP for k in range(2 * KD)]:
                nc.vector.memset(idxT[:, c + INTER:c + OCP], -1.0)
            nc.vector.memset(idxT[:, DOWN0 + (OC - 1) * D:], -1.0)
            own()
            turn[0] = 0
            IDX = []
            for src_col in (0, UP0):
                for oc in range(OC):
                    rows = P if oc < OC - 1 else LAST
                    IDX.append((rows, [(src_col + k * OCP + oc * P, rows, P, k) for k in range(KD)]))
            for hb in range(KD):
                IDX.append((P, [(DOWN0 + oc * D + hb * P, P, P if oc < OC - 1 else LAST, oc) for oc in range(OC)]))
            seq = 0
            for m, (rows, blocks) in enumerate(IDX):
                wide = INTER if m >= 2 * OC else D
                dve.wait_ge(idx_in[m % 2], n(idx_in[m % 2], 16))
                nc.vector.tensor_copy(idx_bf[0:rows, 0:wide], idx_i[0:rows, m % 2, 0:wide]).then_inc(idx_cast, 1)
                if m + 2 < len(IDX):
                    signal(idx_used)
                for col, cols, prt, k in blocks:
                    seq += 1
                    dve.wait_ge(idx_bank, seq)
                    last = nc.vector.tensor_copy(idxT[0:prt, col:col + cols],
                                                 MISC[seq % 2][0:prt, 0:cols // 2].bitcast(BF16))
                    last.then_inc(idx_bank_free, 1)
            for f in range(NF):
                fill_part(f)
            cut_maxima()
            NB = 1
            n_part()
            dve.sem_inc(picked_free, 3)
            for i in range(2):
                dve.sem_inc(x2_stored[i], 16)
            n.settle()

            def body(b, nxt):
                jobs = place_jobs(nxt)
                step = 0

                def job_part(job):
                    kind = job[0]
                    if kind == "T":
                        t_part(job[1])
                    elif kind == "N":
                        n_part()
                    elif kind == "C":
                        _, g, qc = job
                        dve.wait_ge(misc_dve, n(misc_dve))
                        o = ms[:, 0:2 * P].rearrange("p (t h c) -> p t h c", t=2, h=GH)
                        nc.vector.reciprocal(rden[:, :, :], o[:, :, :, HD])
                        own()
                        nc.vector.tensor_tensor(
                            attn[:, 2 * qc:2 * qc + 2, g * GH * HD:(g + 1) * GH * HD].rearrange("p t (h c) -> p t h c", h=GH),
                            o[:, :, :, 0:HD], rden[:, :, :].unsqueeze(3).broadcast_to([P, 2, GH, HD]),
                            ALU.mult).then_inc(misc_free[0], 1)
                    elif kind == "OP":
                        t = job[1]
                        dve.wait_ge(x2_stored[t % 2], n(x2_stored[t % 2], 16))
                        dve.wait_ge(xres_in[t % 2], n(xres_in[t % 2], 16))
                        dve.wait_ge(misc_dve, n(misc_dve))
                        nc.vector.tensor_tensor(x2t[:, t % 2, :], ms[:, 0:D], xres[:, t % 2, :],
                                                ALU.add).then_inc(misc_free[0], 1)
                        signal(x2_ready)

                for u in range(NG * NU):
                    g, l = divmod(u, NU)
                    for job in jobs[u - 1] if u else []:
                        job_part(job)
                    for job in jobs[u - 2] if u >= 2 else []:
                        if job == ("QK", 0):
                            qk_norm(0)
                    if l < FILL_UNITS and (nxt or g < NG - 1):
                        for f in range(PER * l, PER * (l + 1)):
                            fill_part(f)
                        if l == FILL_UNITS - 1:
                            cut_maxima()
                    if nxt and u == STATS_UNIT:
                        batch_stats()
                    for job in jobs.get(u + 1, []):
                        if job[0] == "X":
                            norm_tile(job[1])
                    if nxt and FILL_UNITS <= l < FILL_UNITS + 6:
                        for _ in range(2):
                            i, j = step % LUTB, step // LUTB
                            dve.wait_ge(picked_free, n(picked_free))
                            nc.vector.tensor_scalar(picked[:, step % 3, :], idxT[:, bass.ds((b * LUTB + i) * BANK, BANK)],
                                                    float(j), lut_sb[:, j:j + 1], ALU.is_equal,
                                                    ALU.mult).then_inc(picked_ready, 1)
                            step += 1
                for job in jobs[NG * NU - 1] + TAIL:
                    job_part(job)
                n.settle()

            with dve.Fori(0, B - 1) as b:
                body(b, True)
            body(B - 1, False)

            for i in range(2):
                dve.wait_ge(x2_stored[i], n(x2_stored[i], 16))
            dve.wait_ge(lut_done, 1)
            signal(stacks_read)
            signal(f_x2_used)
            signal(f_x2_used)

            def chunk_stats(c):
                dve.wait_ge(f_x2_in[c], n(f_x2_in[c], 16))
                row_stats([x2f[:, c, t, :] for t in range(TC)])

            def norm_rows(c):
                dve.wait_ge(rstd_ready, n(rstd_ready))
                for t in range(TC):
                    normed(xnf[:, t, :], x2f[:, c, t, :], t).then_inc(f_xn_ready, 1)

            def x_low(c, p):
                dve.wait_ge(f_xhi_ready, n(f_xhi_ready))
                cols = slice(2 * p * P, 2 * (p + 1) * P)
                nc.vector.tensor_tensor(xTl[:, c, :, cols].rearrange("p k (t r) -> p t k r", t=2),
                                        TB[p].rearrange("p (t k r) -> p t k r", t=2, k=KD),
                                        xTh[:, c, :, cols].rearrange("p k (t r) -> p t k r", t=2).bitcast(F32),
                                        ALU.subtract).then_inc(f_xT_ready, 1)

            for i in range(2):
                dve.sem_inc(f_stored[i], 16)
            chunk_stats(0)
            norm_rows(0)
            dve.wait_ge(f_w_hi, 1)
            nc.vector.tensor_tensor(wlo[:, :], wlook[:, :], whi[:, :].bitcast(F32), ALU.subtract).then_inc(f_w_ready, 1)
            x_low(0, 0)
            x_low(0, 1)
            n.settle()

            def ffn_pair(more):
                for c in range(2):
                    ahead = more or c == 0
                    for oc in range(OC):
                        if ahead and oc == 0:
                            chunk_stats(1 - c)
                        if ahead and oc == 1:
                            norm_rows(1 - c)
                        dve.wait_ge(f_silu_ready, n(f_silu_ready))
                        nc.vector.tensor_tensor(hf[:, oc % 2, :], silu[:, oc % 2, :], UB[oc % 2], ALU.mult)
                        nc.vector.tensor_tensor(hhi[:, oc, :], silu[:, oc % 2, :], UB[oc % 2],
                                                ALU.mult).then_inc(f_gu_free, 1)
                        own()
                        nc.vector.tensor_tensor(hlo[:, oc, :], hf[:, oc % 2, :], hhi[:, oc, :].bitcast(F32),
                                                ALU.subtract).then_inc(f_h_ready, 1)
                        if ahead and oc in (2, 4):
                            x_low(1 - c, oc // 2 - 1)
                    for t in range(TC):
                        dve.wait_ge(f_stored[t % 2], n(f_stored[t % 2], 16))
                        dve.wait_ge(f_y_ready, n(f_y_ready))
                        nc.vector.tensor_tensor(yt[:, t % 2, :], YB[t % 2][:, 0:D], x2f[:, c, t, :],
                                                ALU.add).then_inc(f_y_free, 1)
                        signal(f_out_ready)
                    if more:
                        signal(f_x2_used)
                n.settle()

            with dve.Fori(0, NCHUNK // 2 - 1) as i:
                ffn_pair(True)
            ffn_pair(False)
            for i in range(2):
                dve.wait_ge(f_stored[i], n(f_stored[i], 16))

        @block.tensor
        def _(pe):
            n = Tally(pe)

            def misc_turn(k):
                pe.wait_ge(misc_free[k], n(misc_free[k]))
                return MISC[k]

            turn = [0]
            NB = 4

            def bank():
                k = turn[0] % NB
                turn[0] += 1
                return k

            xnT_at = {}

            def evacuated(k):
                pe.wait_ge(misc_free[k], n.count(misc_free[k]) + 1)

            def transpose_rows(t):
                k = bank()
                m = misc_turn(k)
                pe.wait_ge(xn_ready, n(xn_ready))
                for h in range(KD):
                    last = nc.tensor.transpose(m[:, h * P:(h + 1) * P], xn[:, t % 2, h * P:(h + 1) * P], ident[:, :])
                last.then_inc(misc_act, 1)
                xnT_at[t] = k

            def project(t, c0, c1, done):
                k = bank()
                m = misc_turn(k)
                w = c1 - c0
                nc.tensor.matmul(m[:, 0:w], ones3[:, :], bias[:, c0:c1], start=True, stop=False)
                for h in range(KD):
                    last = nc.tensor.matmul(m[:, 0:w], xnT[:, h, t * P:(t + 1) * P], wqkv[:, h, c0:c1],
                                            start=False, stop=h == KD - 1)
                    if h == 0 and done is None:
                        last.then_inc(xn_free, 1)
                last.then_inc(misc_act, 1)

            def qk(t):
                evacuated(xnT_at[t])
                project(t, 0, 2 * D, None)

            def transpose_qk(t):
                k = bank()
                m = misc_turn(k)
                pe.wait_ge(qkn_ready, n(qkn_ready))
                for a in range(4):
                    last = nc.tensor.transpose(m[:, a * P:(a + 1) * P], qkn[:, a * P:(a + 1) * P], ident[:, :])
                last.then_inc(misc_act, 1)

            def fill(f, g):
                pe.wait_ge(fill_free, n(fill_free))
                h, pieces = f // len(FILLS), FILLS[f % len(FILLS)]
                for qt, k0, w, col, _ in pieces:
                    last = nc.tensor.matmul(mx[:, f % 2, col:col + w], qs[g][0:KROWS, h, qt * P:(qt + 1) * P],
                                            ks[g][0:KROWS, h, k0:k0 + w], start=True, stop=True)
                last.then_inc(fill_ready, 1)

            def transpose_maxima():
                k = bank()
                m = misc_turn(k)
                pe.wait_ge(mcut_ready, n(mcut_ready))
                nc.tensor.transpose(m[0:96, 0:P // 2].bitcast(BF16), mcut[:, :, :].rearrange("p a c -> p (a c)"),
                                    identb[:, :]).then_inc(misc_dve, 1)

            def scores(g, l, u):
                qc, kt = UNITS[l]
                w = width(l)
                q0 = (qc + 1) * QC - w
                if l == 0:
                    pe.wait_ge(shift_ready, n(shift_ready, 48))
                for h in range(GH):
                    last = nc.tensor.matmul(sc[:, u % 2, h, 0:w], ks[g][0:SROWS, h, kt * P:(kt + 1) * P],
                                            qs[g][0:SROWS, h, q0:q0 + w], start=True, stop=True)
                last.then_inc(sc_ready, 1)

            pe.sem_inc(fill_free, 2)
            for k in range(4):
                pe.sem_inc(misc_free[k], 1)

            pe.wait_ge(made, 1)
            pe.wait_ge(weights_in, 16 * 2)
            pe.wait_ge(bias_placed, 48)
            for kind, t in ORDER:
                {"X": transpose_rows, "QK": qk, "T": transpose_qk}[kind](t)
            for k in range(NB):
                evacuated(k)
            n.settle()
            seq = 0
            for m in range(2 * OC + KD):
                pe.wait_ge(idx_cast, m + 1)
                blocks = KD if m < 2 * OC else OC
                rows = LAST if m < 2 * OC and m % OC == OC - 1 else P
                for kb in range(blocks):
                    cols = LAST if m >= 2 * OC and kb == OC - 1 else P
                    if seq >= 2:
                        pe.wait_ge(idx_bank_free, seq - 1)
                    seq += 1
                    nc.tensor.transpose(MISC[seq % 2][0:cols, 0:rows // 2].bitcast(BF16),
                                        idx_bf[0:rows, kb * P:kb * P + cols], identb[0:rows, 0:rows]).then_inc(idx_bank, 1)
            pe.wait_ge(idx_bank_free, seq)
            pe.wait_ge(stack_ready[0], n(stack_ready[0], 2 * NTERM * 16))
            for f in range(NF):
                fill(f, 0)
            NB, turn[0] = 1, 0
            transpose_maxima()
            scores(0, 0, 0)
            scores(0, 1, 1)
            n.settle()

            def body(b, nxt):
                jobs = place_jobs(nxt)
                total = NG * NU

                def job_part(job):
                    kind = job[0]
                    if kind == "V":
                        project(job[1], 2 * D, 3 * D, misc_act)
                    elif kind == "X":
                        transpose_rows(job[1])
                    elif kind == "QK":
                        qk(job[1])
                    elif kind == "T":
                        if job[1] == 0:
                            pe.wait_ge(stack_ready[NG - 1], n(stack_ready[NG - 1], 2 * NTERM * 16))
                        transpose_qk(job[1])
                    elif kind == "N":
                        transpose_maxima()
                    elif kind == "C":
                        _, g, qc = job
                        m = misc_turn(bank())
                        for i in range(2):
                            last = nc.tensor.transpose(m[:, i * P:(i + 1) * P],
                                                       oT[:, (g * NQC + qc) % 2, i * P:(i + 1) * P], ident[:, :])
                        last.then_inc(misc_dve, 1)
                    elif kind == "OT":
                        m = misc_turn(bank())
                        for i in range(2):
                            for k in range(KD):
                                last = nc.tensor.transpose(m[:, (i * KD + k) * P:(i * KD + k + 1) * P],
                                                           attn[:, 2 * job[1] + i, k * P:(k + 1) * P], ident[:, :])
                        last.then_inc(misc_act, 1)
                    elif kind == "OP":
                        m = misc_turn(bank())
                        nc.tensor.matmul(m[:, 0:D], ones3[:, :], bias[:, 3 * D:], start=True, stop=False)
                        for k in range(KD):
                            last = nc.tensor.matmul(m[:, 0:D], attnT[:, job[1] % 2, k, :], wout[:, k, :],
                                                    start=False, stop=k == KD - 1)
                        last.then_inc(misc_dve, 1)

                for u in range(total):
                    g, l = divmod(u, NU)
                    if l < FILL_UNITS and (nxt or g < NG - 1):
                        nextg = (g + 1) % NG
                        if l == 0 and not (nextg == NG - 1 and nxt):
                            pe.wait_ge(stack_ready[nextg], n(stack_ready[nextg], 2 * NTERM * 16))
                        for f in range(PER * l, PER * (l + 1)):
                            fill(f, nextg)
                    for job in jobs[u]:
                        job_part(job)
                    if is_diag(l):
                        pe.wait_ge(masked, n(masked))
                    else:
                        pe.wait_ge(exp_full, n(exp_full))
                    if u + 2 < total:
                        scores((u + 2) // NU, (u + 2) % NU, u + 2)
                    elif nxt:
                        scores(0, (u + 2) % NU, u + 2)
                    if g == 0 and u < 8:
                        evacuated(0)
                    qc, kt = UNITS[l]
                    if kt == 0 and u > 0:
                        pe.wait_ge(oT_ready, n(oT_ready))
                    w = width(l)
                    for h in range(GH):
                        last = nc.tensor.matmul(ov[32 * h:32 * (h + 1), QC - w:QC],
                                                vaug[:, kt, g * GH + h, :], probs[:, u % 2, h, 0:w],
                                                start=kt == 0, stop=kt == 2 * qc + 1)
                        if h == 0 and l == NU - 3:
                            last.then_inc(stack_free, 1)
                    last.then_inc(av_done, 1)
                pe.wait_ge(oT_ready, n(oT_ready))
                for job in TAIL:
                    job_part(job)
                n.settle()

            with pe.Fori(0, B - 1) as b:
                body(b, True)
            body(B - 1, False)

            pe.wait_ge(fill_free, 2)
            pe.wait_ge(misc_free[0], 1)

            def transpose_pair(c, p):
                for i in range(2):
                    t = 2 * p + i
                    pe.wait_ge(f_xn_ready, n(f_xn_ready))
                    for k in range(KD):
                        last = nc.tensor.transpose(TB[p][:, (i * KD + k) * P:(i * KD + k + 1) * P],
                                                   xnf[:, t, k * P:(k + 1) * P], ident[:, :])
                last.then_inc(f_tr_ready, 1)

            transpose_pair(0, 0)
            transpose_pair(0, 1)
            pe.wait_ge(f_w_ready, 1)
            pe.wait_ge(f_xT_ready, n(f_xT_ready, 2))
            pe.sem_inc(f_gu_free, 2)
            pe.sem_inc(f_y_free, 2)
            n.settle()

            def weight(at, width, high):
                return (whi if high else wlo)[:, at:at + width]

            def ffn_pair(more):
                for c in range(2):
                    ahead = more or c == 0
                    for oc in range(OC):
                        pe.wait_ge(f_gu_free, n(f_gu_free))
                        for col0, dst in ((0, GB[oc % 2]), (UP0, UB[oc % 2])):
                            terms = [(k, wh, xh) for k in range(KD) for wh, xh in ((1, 1), (0, 1), (1, 0))]
                            for i, (k, wh, xh) in enumerate(terms):
                                last = nc.tensor.matmul(dst, weight(col0 + k * OCP + oc * P, P, wh), (xTh if xh else xTl)[:, c, k, :],
                                                        start=i == 0, stop=i == len(terms) - 1)
                        last.then_inc(f_gu_ready, 1)
                        if ahead and oc in (1, 3):
                            transpose_pair(1 - c, oc // 2)
                    for p in range(TC // 2):
                        for pieces in (range(OC - 1), range(OC - 1, OC)):
                            for i in range(2):
                                t = 2 * p + i
                                if 0 in pieces:
                                    pe.wait_ge(f_y_free, n(f_y_free))
                                for oc in pieces:
                                    if t == 0:
                                        pe.wait_ge(f_h_ready, n(f_h_ready))
                                    for j, (hh, wh) in enumerate(((1, 1), (0, 1), (1, 0))):
                                        last = nc.tensor.matmul(YB[i][:, 0:D], (hhi if hh else hlo)[:, oc, t * P:(t + 1) * P],
                                                                weight(DOWN0 + oc * D, D, wh), start=oc == 0 and j == 0,
                                                                stop=oc == OC - 1 and j == 2)
                                if OC - 1 in pieces:
                                    last.then_inc(f_y_ready, 1)
                    if ahead:
                        pe.wait_ge(f_xT_ready, n(f_xT_ready, 2))
                n.settle()

            with pe.Fori(0, NCHUNK // 2 - 1) as i:
                ffn_pair(True)
            ffn_pair(False)


_INS = ['L0_attn_x', 'L0_attn_w_qkv', 'L0_attn_b_qkv', 'L0_attn_q_ln_w', 'L0_attn_k_ln_w', 'L0_attn_w_out',
        'L0_attn_b_out', 'L0_ffn_lut', 'L0_ffn_gate_idx', 'L0_ffn_up_idx', 'L0_ffn_down_idx']


def kernel(**inputs):
    import numpy as _np
    import concourse.bacc as _bacc
    from concourse import mybir as _mybir
    from concourse.bass_utils import run_bass_kernel_spmd as _run

    nc = _bacc.Bacc("TRN2", target_bir_lowering=False, num_devices=1)
    arrays, args = {}, []
    for name in _INS:
        a = _np.ascontiguousarray(inputs[name])
        arrays[f"in_{name}_dram"] = a
        args.append(nc.dram_tensor(f"in_{name}_dram", a.shape, _mybir.dt.from_np(a.dtype), kind="ExternalInput").ap())
    shape = inputs['L0_attn_x'].shape
    args.append(nc.dram_tensor("out_0_dram", shape, _mybir.dt.float32, kind="ExternalOutput").ap())
    layer_kernel(nc, *args)
    r = _run(nc, [arrays], core_ids=[0])
    return r.results[0]["out_0_dram"]
```

```python
import struct
from contextlib import ExitStack

import concourse.bass as bass
from concourse import mybir

F32 = mybir.dt.float32
F32R = mybir.dt.float32r
BF16 = mybir.dt.bfloat16
I32 = mybir.dt.int32
ALU = mybir.AluOpType
ACT = mybir.ActivationFunctionType
AX_X = mybir.AxisListType.X

P = 128
BANK = 512
MASKED = -1.0e30
LEAST = -3.0e38
TWO_ONES = struct.unpack("<f", struct.pack("<I", 0x3F803F80))[0]


class Tally:

    def __init__(self, eng):
        self.eng, self.seen = eng, {}

    def __call__(self, sem, by=1):
        name = sem.name
        self.seen[name] = (sem, self.seen.get(name, (sem, 0))[1] + by)
        return self.seen[name][1]

    def count(self, sem):
        return self.seen.get(sem.name, (sem, 0))[1]

    def settle(self):
        self.eng.drain()
        for sem, n in self.seen.values():
            self.eng.sem_inc(sem, -n)
        self.seen = {}


def layer_kernel(nc, x, w_qkv, b_qkv, q_ln_w, k_ln_w, w_out, b_out, lut, gate_idx, up_idx, down_idx, out):
    B, S, D = x.shape
    H = 16
    HD = D // H
    INTER = gate_idx.shape[0]
    NLUT = lut.shape[0]
    KD = D // P
    RT = S // P
    GH = 4
    NG = H // GH
    QC = 256
    NQC = S // QC
    NTERM = 6
    Q_PART = [0, 0, 0, 1, 1, 2]
    K_PART = [0, 1, 2, 0, 1, 0]
    KROWS = NTERM * HD
    SROWS = KROWS + 3
    OC = (INTER + P - 1) // P
    OCP = OC * P
    LAST = INTER - (OC - 1) * P
    WCOLS = 2 * KD * OCP + OC * D
    UP0, DOWN0 = KD * OCP, 2 * KD * OCP
    NCH = WCOLS // BANK
    LUTB = NCH // (B - 1)
    assert S == 4 * D and NCH % (B - 1) == 0 and RT == 8 and KD == 2 and D == 256
    CH = 512
    NCHUNK = B * S // CH
    TC = CH // P

    UNITS = [(qc, kt) for qc in range(NQC) for kt in range(2 * qc + 2)]
    NU = len(UNITS)
    CHUNK_END = {UNITS.index((qc, 2 * qc + 1)): qc for qc in range(NQC)}

    def is_diag(l):
        qc, kt = UNITS[l]
        return kt >= 2 * qc

    def width(l):
        qc, kt = UNITS[l]
        return P if kt == 2 * qc + 1 else QC

    FILLS = [
        [(0, 0, 128, 0, True), (2, 0, 384, 128, True)],
        [(3, 0, 512, 0, True)],
        [(4, 0, 512, 0, False)],
        [(5, 0, 512, 0, False)],
        [(6, 0, 512, 0, False)],
        [(7, 0, 512, 0, False)],
        [(4, 512, 128, 0, True), (6, 512, 384, 128, True)],
        [(7, 512, 512, 0, True)],
        [(1, 0, 256, 0, True), (5, 512, 256, 256, True)],
    ]
    NF = len(FILLS) * GH
    FILL_LEAD = 6

    def fill_unit(group, f):
        return NU * (group - 1) - FILL_LEAD + f * NU // NF

    def fills_of(u, nxt):
        groups = range(1, NG + 2 if nxt else NG)
        return [(g, f) for g in groups for f in range(NF) if fill_unit(g, f) == u]

    EARLY = [f for f in range(NF) if fill_unit(1, f) < 0]
    CUT_UNIT = NU - FILL_LEAD - 1

    ORDER = []
    for t in range(RT + 1):
        if t < RT:
            ORDER += [("X", t), ("QK", t)]
        if t:
            ORDER.append(("T", t - 1))
    STATS_UNIT = 4

    EARLY_V = 2

    LUT_UNITS = [l for l in range(NU) if not is_diag((l + 1) % NU)]
    assert len(LUT_UNITS) * NG == NLUT * LUTB

    def place_jobs(nxt):
        jobs = {u: [] for u in range(NG * NU)}
        for t, u in zip(range(EARLY_V, RT), [0, 1, 3, 5, 6, 7], strict=True):
            jobs[u].append(("V", t))
        for g in range(NG):
            for l, qc in CHUNK_END.items():
                u = NU * g + l + (4 if qc == NQC - 2 else 3)
                if u < NG * NU:
                    jobs[u].append(("C", g, qc))
            if g < NG - 1 or nxt:
                jobs[NU * g + CUT_UNIT + 1].append(("N", (g + 1) % NG))
        if nxt:
            free = [u for u in range(STATS_UNIT + 4, 3 * NU - FILL_LEAD - 8) if not jobs[u]]
            for u, job in zip(free, ORDER, strict=False):
                jobs[u].append(job)
            assert len(free) >= len(ORDER)
        g0 = (NG - 1) * NU
        for u, job in [(5, ("OT", 0)), (6, ("OP", 0)), (7, ("OP", 1)), (9, ("OT", 1)), (10, ("OP", 2)),
                       (11, ("OP", 3)), (16, ("OT", 2)), (17, ("OP", 4)), (18, ("OP", 5))]:
            jobs[g0 + u].append(job)
        if nxt:
            jobs[g0 + 13].append(("V", 0))
            jobs[g0 + 19].append(("V", 1))
        assert all(len(j) == 1 for j in jobs.values() if j)
        return jobs

    NRING = 3

    def turns(uses):
        return {use: i % NRING for i, use in enumerate(uses)}

    def unit_uses(u, nxt):
        fills = [("fill", g, f) for g, f in fills_of(u, nxt)]
        return fills[:1] + place_jobs(nxt)[u] + fills[1:]

    TAIL = [("C", NG - 1, NQC - 1), ("OT", 3), ("OP", 6), ("OP", 7)]
    START_TURNS = turns([("fill", 0, f) for f in range(NF)] + [("N", 0)] + [("V", t) for t in range(EARLY_V)]
                        + [("fill", 1, f) for f in EARLY])
    BODY_TURNS = {nxt: turns([use for u in range(NG * NU) for use in unit_uses(u, nxt)] + TAIL) for nxt in (True, False)}

    with ExitStack() as ctx:
        def sb(name, shape, dt=F32):
            return ctx.enter_context(nc.sbuf_tensor(name, shape, dt))

        def sem(name):
            return ctx.enter_context(nc.semaphore(name))

        ident = sb("ident", [P, P])
        identb = sb("identb", [P, P], BF16)
        causal = sb("causal", [P, BANK], BF16)
        wqkv = sb("wqkv", [P, KD, 3 * D])
        wout = sb("wout", [P, KD, D])
        lnw = sb("lnw", [P, 2 * D])
        bias = sb("bias", [3, 4 * D], BF16)
        ones3 = sb("ones3", [3, P], BF16)
        lut_sb = sb("lut_sb", [P, NLUT])
        xin = sb("xin", [P, RT, D])
        xn = sb("xn", [P, 2, D])
        xnT = sb("xnT", [P, KD, S])
        stats = sb("stats", [P, RT, 6])
        mv = sb("mv", [P, RT, 2])
        var = sb("var", [P, RT])
        rstd = sb("rstd", [P, RT])
        minus_half = sb("minus_half", [P, RT])
        ss = sb("ss", [P, 2, 2])
        sse = sb("sse", [P, 2, 2])
        rs = sb("rs", [P, 2, 2])
        probs = sb("probs", [P, 2, GH, QC])
        maxj = sb("maxj", [P, NRING, BANK], BF16)
        mdiag = sb("mdiag", [P, GH * RT])
        mfull = sb("mfull", [P, GH * RT])
        mrow = sb("mrow", [P, GH * RT])
        mrest = sb("mrest", [P, 2, GH * RT])
        mcut = sb("mcut", [P, 3, GH * RT], BF16)
        mcutT = sb("mcutT", [P, P], BF16)
        oT = sb("oT", [P, 2, QC])
        rden = sb("rden", [P, 2, 2, GH])
        attn = sb("attn", [P, RT, D])
        attnT = sb("attnT", [P, 2, KD, P])
        xres = sb("xres", [P, 2, D])
        x2t = sb("x2t", [P, 2, D])
        idxT = sb("idxT", [P, WCOLS], BF16)
        wlook = sb("wlook", [P, WCOLS])
        picked = sb("picked", [P, 2, BANK])
        with ExitStack() as attention:
            def sba(name, shape, dt=F32):
                return attention.enter_context(nc.sbuf_tensor(name, shape, dt))

            sqj = sba("sqj", [P, 2, D], BF16)
            qkraw = sba("qkraw", [P, 2, 2 * D])
            qkn = sba("qkn", [P, 2 * D])
            parts = sba("parts", [P, 3, 4, S], BF16)
            rest = sba("rest", [P, 2, BANK])
            qs = [sba(f"qs{g}", [P, GH, S], BF16) for g in range(NG)]
            ks = [sba(f"ks{g}", [P, GH, S], BF16) for g in range(NG)]
            vaug = sba("vaug", [P, RT, H, 32])
        whi = sb("whi", [P, WCOLS], F32R)
        wlo = sb("wlo", [P, WCOLS], F32R)
        xTh = sb("xTh", [P, 2, KD, CH], F32R)
        xTl = sb("xTl", [P, 2, KD, CH], F32R)
        hhi = sb("hhi", [P, OC, CH], F32R)
        hlo = sb("hlo", [P, OC, CH], F32R)
        parts_dram = nc.dram_tensor("parts_scratch", (3, 4, P, S), BF16, kind="Internal").ap()
        x2_dram = nc.dram_tensor("x2_scratch", (B * S, D), F32, kind="Internal").ap()

        sc = ctx.enter_context(nc.psum_tensor("sc", [P, 2, GH, QC], F32))
        mx = ctx.enter_context(nc.psum_tensor("mx", [P, 2, BANK], F32))
        ov = ctx.enter_context(nc.psum_tensor("ov", [P, BANK], F32))
        ms = ctx.enter_context(nc.psum_tensor("ms", [P, BANK], F32))
        scf = sc[:].rearrange("p a h q -> p (a h q)")
        PROLOGUE = [ms[:, :]] + [scf[:, BANK * i:BANK * (i + 1)] for i in range(3)]
        RING = [ms[:, :], mx[:, 0, :], mx[:, 1, :]]

        class Banks:

            def __init__(self):
                self.turn, self.turns = 0, None

            def of(self, *use):
                if self.turns is None:
                    k = self.turn % len(PROLOGUE)
                    self.turn += 1
                    return k, PROLOGUE[k]
                k = self.turns[use]
                return k, RING[k]

        bias_in, consts_in, weights_in, x_in = sem("bias_in"), sem("consts_in"), sem("weights_in"), sem("x_in")
        bias_cut_ready, bias_placed, made = sem("bias_cut_ready"), sem("bias_placed"), sem("made")
        vaug_made = sem("vaug_made")
        idx_in, idx_used = [sem("idx_in0"), sem("idx_in1")], sem("idx_used")
        idx_cast, idx_bank, idx_bank_free = sem("idx_cast"), sem("idx_bank"), sem("idx_bank_free")
        xin_used = sem("xin_used")
        xn_ready, xn_free = sem("xn_ready"), sem("xn_free")
        bank_free = [sem(f"bank_free{i}") for i in range(4)]
        misc_act, misc_dve = sem("misc_act"), sem("misc_dve")
        var_ready, rstd_ready = sem("var_ready"), sem("rstd_ready")
        ss_ready, rs_ready, qkn_ready = sem("ss_ready"), sem("rs_ready"), sem("qkn_ready")
        p1_ready, r1_ready, p2_ready, rest_free = sem("p1_ready"), sem("r1_ready"), sem("p2_ready"), sem("rest_free")
        parts_ready, parts_stored = sem("parts_ready"), sem("parts_stored")
        stack_ready = [sem(f"stack_ready{g}") for g in range(NG)]
        stack_free = sem("stack_free")
        fill_ready = sem("fill_ready")
        mcut_ready, mcutT_ready = sem("mcut_ready"), sem("mcutT_ready")
        shift_ready = sem("shift_ready")
        sc_ready = sem("sc_ready")
        exp_done, exp_diag, masked = sem("exp_done"), sem("exp_diag"), sem("masked")
        av_done, oT_ready = sem("av_done"), sem("oT_ready")
        xres_in = [sem("xres_in0"), sem("xres_in1")]
        x2_ready = sem("x2_ready")
        x2_stored = [sem("x2_stored0"), sem("x2_stored1")]
        picked_ready, picked_free, lut_done = sem("picked_ready"), sem("picked_free"), sem("lut_done")
        dve_self, pool_self = sem("dve_self"), sem("pool_self")
        f_x2_in = [sem("f_x2_in0"), sem("f_x2_in1")]
        f_x2_used = sem("f_x2_used")
        f_w_ready, f_w_hi = sem("f_w_ready"), sem("f_w_hi")
        stacks_read = sem("stacks_read")
        f_xn_ready = sem("f_xn_ready")
        f_tr_ready, f_xhi_ready, f_xT_ready = sem("f_tr_ready"), sem("f_xhi_ready"), sem("f_xT_ready")
        f_gu_ready, f_silu_ready, f_gu_free, f_h_ready = sem("f_gu_ready"), sem("f_silu_ready"), sem("f_gu_free"), sem("f_h_ready")
        f_y_ready, f_y_free, f_out_ready = sem("f_y_ready"), sem("f_y_free"), sem("f_out_ready")
        f_stored = [sem("f_stored0"), sem("f_stored1")]

        x_rows = x.rearrange("b (t p) d -> b p t d", p=P)
        x_flat = x.rearrange("b s d -> (b s) d")
        out_flat = out.rearrange("b s d -> (b s) d")

        x2f = xin[:, :, :].rearrange("p (c t) d -> p c t d", c=2)
        silu = probs[:, :, :, :].rearrange("p a h q -> p a (h q)")[:, :, 0:CH]
        hf = xnT[:, :, 0:CH]
        yt = x2t
        xnf = attn[:, 0:TC, :]
        idx_i = probs[:, :, :, :].rearrange("p a h q -> p a (h q)").bitcast(I32)
        bias_row = attn[0:3, 0:4, :].rearrange("p a d -> p (a d)")
        bias_rest = attn[0:3, 4:8, :].rearrange("p a d -> p (a d)")
        bias_cut = parts[0:3, :, 0, :]
        idx_bf = oT[:, :, :].rearrange("p a q -> p (a q)").bitcast(BF16)
        GB = [scf[:, 0:BANK], scf[:, BANK:2 * BANK]]
        UB = [scf[:, 2 * BANK:3 * BANK], scf[:, 3 * BANK:4 * BANK]]
        YB = [mx[:, 0, :], mx[:, 1, :]]
        TB = [ov[:, :], ms[:, :]]

        block = ctx.enter_context(nc.Block())

        @block.sync
        def _(sp):
            n = Tally(sp)
            sp.dma_start(bias_row[:, 0:3 * D], b_qkv.partition_broadcast(3)).then_inc(bias_in, 16)
            sp.dma_start(bias_row[:, 3 * D:], b_out.partition_broadcast(3)).then_inc(bias_in, 16)
            sp.dma_start(xin[:, :, :], x_rows[0]).then_inc(x_in, 16)
            sp.dma_start(wqkv[:, :, :], w_qkv.rearrange("(k p) n -> p k n", p=P)).then_inc(weights_in, 16)
            sp.wait_ge(bias_cut_ready, 1)
            for i in range(3):
                sp.dma_start(bias[i:i + 1, :], bias_cut[i:i + 1, i, :]).then_inc(bias_placed, 16)
            sp.dma_start(lnw[:, 0:D], q_ln_w.partition_broadcast(P)).then_inc(consts_in, 16)
            sp.dma_start(lnw[:, D:], k_ln_w.partition_broadcast(P)).then_inc(consts_in, 16)
            sp.dma_start(wout[:, :, :], w_out.rearrange("(k p) n -> p k n", p=P)).then_inc(weights_in, 16)
            sp.dma_start(lut_sb[:, :], lut.partition_broadcast(P)).then_inc(consts_in, 16)

            def parts_out(half):
                sp.wait_ge(parts_ready, n(parts_ready))
                cols = slice(half * S // 2, (half + 1) * S // 2)
                sp.dma_start(parts_dram[:, :, :, cols].rearrange("i a p s -> p i a s"),
                             parts[:, :, :, cols]).then_inc(parts_stored, 16)
                if half == 1:
                    sp.wait_ge(parts_stored, n(parts_stored, 32))

            def stack(g):
                p0 = (g % 2) * (GH * HD)
                for dst, half, terms in ((qs[g], g // 2, Q_PART), (ks[g], 2 + g // 2, K_PART)):
                    for j, part in enumerate(terms):
                        sp.dma_start(dst[HD * j:HD * (j + 1), :, :],
                                     parts_dram[part, half, p0:p0 + GH * HD, :].rearrange("(h d) s -> d h s", h=GH)
                                     ).then_inc(stack_ready[g], 16)

            def shift(g):
                sp.wait_ge(mcutT_ready, n(mcutT_ready))
                for i in range(3):
                    sp.dma_start(qs[g][KROWS + i:KROWS + i + 1, :, :].rearrange("p h (t n) -> p (h t) n", n=P),
                                 mcutT[32 * i:32 * (i + 1), :]).then_inc(shift_ready, 16)

            sp.sem_inc(stack_free, 1)
            parts_out(0)
            parts_out(1)
            for g in range(NG - 1):
                stack(g)
            shift(0)

            def body(b, nxt):
                if nxt:
                    sp.wait_ge(xin_used, n(xin_used))
                    sp.dma_start(xin[:, :, :], x_rows[b + 1]).then_inc(x_in, 16)
                sp.wait_ge(stack_free, n(stack_free))
                stack(NG - 1)
                shift(1)
                if nxt:
                    parts_out(0)
                shift(2)
                if nxt:
                    sp.wait_ge(stack_free, n(stack_free))
                    parts_out(1)
                    stack(0)
                shift(3)
                if nxt:
                    sp.wait_ge(stack_free, n(stack_free))
                    stack(1)
                    sp.wait_ge(stack_free, n(stack_free))
                    stack(2)
                else:
                    sp.wait_ge(stack_free, n(stack_free, NG - 1))
                r0 = b * S
                for t in range(2):
                    sp.dma_start(xres[:, t, :], x_flat[bass.ds(r0 + t * P, P), :]).then_inc(xres_in[t], 16)
                for t in range(RT):
                    if t == 4 and nxt:
                        shift(0)
                    sp.wait_ge(x2_ready, n(x2_ready))
                    sp.dma_start(x2_dram[bass.ds(r0 + t * P, P), :], x2t[:, t % 2, :]).then_inc(x2_stored[t % 2], 16)
                    if t + 2 < RT:
                        sp.dma_start(xres[:, t % 2, :],
                                     x_flat[bass.ds(r0 + (t + 2) * P, P), :]).then_inc(xres_in[t % 2], 16)
                n.settle()

            n.settle()
            with sp.Fori(0, B - 1) as b:
                body(b, True)
            body(B - 1, False)

            for c in range(2):
                sp.wait_ge(f_x2_used, n(f_x2_used))
                sp.dma_start(x2f[:, c], x2_dram[c * CH:(c + 1) * CH, :].rearrange("(t p) d -> p t d", p=P)
                             ).then_inc(f_x2_in[c], 16)
            n.settle()

            def ffn_pair(i, more):
                for c in range(2):
                    r0 = (2 * i + c) * CH
                    for t in range(TC):
                        sp.wait_ge(f_out_ready, n(f_out_ready))
                        sp.dma_start(out_flat[bass.ds(r0 + t * P, P), :], yt[:, t % 2, :]).then_inc(f_stored[t % 2], 16)
                    if more:
                        sp.wait_ge(f_x2_used, n(f_x2_used))
                        sp.dma_start(x2f[:, c], x2_dram[bass.ds(r0 + 2 * CH, CH), :].rearrange("(t p) d -> p t d", p=P)
                                     ).then_inc(f_x2_in[c], 16)
                n.settle()

            with sp.Fori(0, NCHUNK // 2 - 1) as i:
                ffn_pair(i, True)
            ffn_pair(NCHUNK // 2 - 1, False)

        @block.gpsimd
        def _(pool):
            n = Tally(pool)
            nc.gpsimd.memset(ident[:, :], 0.0).then_inc(pool_self, 1)
            pool.wait_ge(pool_self, 1)
            nc.gpsimd.affine_select(out=ident[:, :], in_=ident[:, :], compare_op=ALU.not_equal, fill=1.0, base=0,
                                    pattern=[[-1, P]], channel_multiplier=1).then_inc(pool_self, 1)
            pool.wait_ge(pool_self, 2)
            nc.gpsimd.tensor_copy(identb[:, :], ident[:, :])
            nc.gpsimd.memset(causal[:, :], 0.0).then_inc(pool_self, 1)
            pool.wait_ge(pool_self, 3)
            tri = causal[:, BANK - P:]
            nc.gpsimd.affine_select(out=tri, in_=tri, compare_op=ALU.is_ge, fill=MASKED, base=0,
                                    pattern=[[-1, P]], channel_multiplier=1)
            nc.gpsimd.memset(minus_half[:, :], -0.5)
            pool.drain().then_inc(made, 1)

            def last_part(t):
                pool.wait_ge(p2_ready, n(p2_ready))
                r = rest[:, t % 2, :].rearrange("p (a r) -> p a r", a=4)
                cols = slice(t * P, (t + 1) * P)
                nc.gpsimd.tensor_tensor(parts[:, 2, :, cols], r, parts[:, 1, :, cols],
                                        ALU.subtract).then_inc(rest_free, 1)
                if t % (RT // 2) == RT // 2 - 1:
                    pool.drain().then_inc(parts_ready, 1)

            def roots_of_rows(m):
                pool.wait_ge(var_ready, n(var_ready))
                nc.gpsimd.tensor_tensor(rstd[:, 0:m], var[:, 0:m], minus_half[:, 0:m], ALU.pow).then_inc(rstd_ready, 1)

            def roots_of_qk(t):
                pool.wait_ge(ss_ready, n(ss_ready))
                nc.gpsimd.tensor_scalar(sse[:, t % 2, :], ss[:, t % 2, :], D * 1e-6, None, ALU.add).then_inc(pool_self, 1)
                pool.wait_ge(pool_self, n(pool_self))
                nc.gpsimd.tensor_tensor(rs[:, t % 2, :], sse[:, t % 2, :], minus_half[:, 0:2],
                                        ALU.pow).then_inc(rs_ready, 1)

            pool.sem_inc(pool_self, -3)
            roots_of_rows(RT)
            for kind, t in ORDER:
                if kind == "QK":
                    roots_of_qk(t)
                elif kind == "T":
                    last_part(t)
            nc.gpsimd.memset(vaug[:, :, :, :].rearrange("p t h c -> p (t h c)"), 0.0).then_inc(pool_self, 1)
            pool.wait_ge(pool_self, n(pool_self))
            nc.gpsimd.memset(vaug[:, :, :, HD:HD + 1], 1.0).then_inc(vaug_made, 1)
            nc.gpsimd.memset(wlook[:, :], 0.0)
            n.settle()

            def body(b, nxt):
                jobs = place_jobs(nxt)
                step = 0
                for u in range(NG * NU):
                    l = u % NU
                    if is_diag(l):
                        pool.wait_ge(exp_diag, n(exp_diag))
                        p = probs[:, u % 2, :, 0:P]
                        nc.gpsimd.affine_select(out=p, in_=p, compare_op=ALU.is_ge, fill=0.0, base=0,
                                                pattern=[[0, GH], [1, P]], channel_multiplier=-1).then_inc(masked, 1)
                    for job in jobs[u - 1] if u else []:
                        if job[0] == "T":
                            last_part(job[1])
                        elif job[0] == "QK":
                            roots_of_qk(job[1])
                    if nxt and u == STATS_UNIT + 1:
                        roots_of_rows(RT)
                    if nxt and l in LUT_UNITS:
                        i = step % LUTB
                        pool.wait_ge(picked_ready, n(picked_ready))
                        w = wlook[:, bass.ds((b * LUTB + i) * BANK, BANK)]
                        nc.gpsimd.tensor_tensor(w, w, picked[:, step % 2, :], ALU.add).then_inc(picked_free, 1)
                        step += 1
                n.settle()

            with pool.Fori(0, B - 1) as b:
                body(b, True)
            body(B - 1, False)
            pool.drain().then_inc(lut_done, 1)
            roots_of_rows(TC)
            n.settle()
            with pool.Fori(0, NCHUNK // 2 - 1) as i:
                roots_of_rows(TC)
                roots_of_rows(TC)
                n.settle()
            roots_of_rows(TC)

        @block.scalar
        def _(act):
            n = Tally(act)

            def signal(s):
                act.drain().then_inc(s, 1)

            def x_part(t):
                act.wait_ge(misc_act, n(misc_act))
                k, m = banks.of("X", t)
                nc.scalar.copy(xnT[:, :, t * P:(t + 1) * P],
                               m[:, 0:D].rearrange("p (k r) -> p k r", k=KD)).then_inc(bank_free[k], 1)

            def v_part(t):
                act.wait_ge(misc_act, n(misc_act))
                k, m = banks.of("V", t)
                nc.scalar.copy(vaug[:, t, :, 0:HD],
                               m[:, 0:D].rearrange("p (h c) -> p h c", h=H)).then_inc(bank_free[k], 1)

            def qk_part(t):
                act.wait_ge(misc_act, n(misc_act))
                k, m = banks.of("QK", t)
                nc.scalar.copy(qkraw[:, t % 2, :], m)
                nc.scalar.activation(sqj[:, 0, :], m[:, 0:D], ACT.Square, accum_out=ss[:, t % 2, 0:1])
                nc.scalar.activation(sqj[:, 1, :], m[:, D:], ACT.Square,
                                     accum_out=ss[:, t % 2, 1:2]).then_inc(ss_ready, 1)
                signal(bank_free[k])

            def t_part(t):
                act.wait_ge(misc_act, n(misc_act))
                k, m = banks.of("T", t)
                nc.scalar.copy(parts[:, 0, :, t * P:(t + 1) * P],
                               m.rearrange("p (a r) -> p a r", a=4)).then_inc(p1_ready, 1)

            def second_part(t):
                act.wait_ge(r1_ready, n(r1_ready))
                nc.scalar.copy(parts[:, 1, :, t * P:(t + 1) * P],
                               rest[:, t % 2, :].rearrange("p (a r) -> p a r", a=4)).then_inc(p2_ready, 1)

            banks = Banks()

            IDX = [(src, oc * P, min(P, INTER - oc * P), D) for src in (gate_idx, up_idx) for oc in range(OC)]
            IDX += [(down_idx, hb * P, P, INTER) for hb in range(KD)]

            def load_indices(m):
                src, r0, rows, wide = IDX[m]
                if m >= 2:
                    act.wait_ge(idx_used, n(idx_used))
                act.dma_start(idx_i[0:rows, m % 2, 0:wide], src[r0:r0 + rows, :]).then_inc(idx_in[m % 2], 16)

            load_indices(0)
            load_indices(1)
            act.wait_ge(made, 1)
            for kind, t in ORDER:
                if kind == "X":
                    x_part(t)
                elif kind == "QK":
                    qk_part(t)
                else:
                    t_part(t)
                    second_part(t)
            for m in range(2, len(IDX)):
                load_indices(m)
            act.wait_ge(vaug_made, 1)
            banks.turns = START_TURNS
            for t in range(EARLY_V):
                v_part(t)
            n.settle()

            def body(b, nxt):
                jobs = place_jobs(nxt)
                banks.turns = BODY_TURNS[nxt]

                def out_chunk(u):
                    act.wait_ge(av_done, u + 1)
                    c = u // NU * NQC + CHUNK_END[u % NU]
                    nc.scalar.copy(oT[:, c % 2, :], ov[:, 0:QC]).then_inc(oT_ready, 1)

                def job_part(job):
                    kind = job[0]
                    if kind == "V":
                        v_part(job[1])
                    elif kind == "X":
                        x_part(job[1])
                    elif kind == "QK":
                        qk_part(job[1])
                    elif kind == "T":
                        t_part(job[1])
                    elif kind == "OT":
                        act.wait_ge(misc_act, n(misc_act))
                        k, m = banks.of(*job)
                        nc.scalar.copy(attnT[:, :, :, :].rearrange("p t k r -> p (t k r)"), m).then_inc(bank_free[k], 1)

                for u in range(NG * NU):
                    l = u % NU
                    if u >= 2:
                        if (l - 2) % NU in CHUNK_END:
                            out_chunk(u - 2)
                        act.wait_ge(av_done, u - 1)
                    n(av_done)
                    act.wait_ge(sc_ready, n(sc_ready))
                    w = width(l)
                    s = sc[:, u % 2, :, 0:w]
                    p = probs[:, u % 2, :, 0:w]
                    nc.scalar.activation(p, s, ACT.Exp).then_inc(exp_done, 1)
                    for job in jobs.get(u - 2, []):
                        if job[0] == "T":
                            second_part(job[1])
                    for job in jobs.get(u - 1, []):
                        job_part(job)
                for job in jobs[NG * NU - 1]:
                    job_part(job)
                out_chunk(NG * NU - 1)
                for job in TAIL:
                    job_part(job)
                n.settle()

            with act.Fori(0, B - 1) as b:
                body(b, True)
            body(B - 1, False)

            def x_high(c, p):
                act.wait_ge(f_tr_ready, n(f_tr_ready))
                nc.scalar.copy(xTh[:, c, :, 2 * p * P:2 * (p + 1) * P].rearrange("p k (t r) -> p t k r", t=2),
                               TB[p].rearrange("p (t k r) -> p t k r", t=2, k=KD)).then_inc(f_xhi_ready, 1)

            act.wait_ge(lut_done, 1)
            act.wait_ge(stacks_read, 1)
            nc.scalar.copy(whi[:, :], wlook[:, :]).then_inc(f_w_hi, 1)
            for p in range(2):
                x_high(0, p)
            n.settle()

            def ffn_pair(more):
                for c in range(2):
                    for oc in range(OC):
                        act.wait_ge(f_gu_ready, n(f_gu_ready))
                        nc.scalar.activation(silu[:, oc % 2, :], GB[oc % 2], ACT.Silu).then_inc(f_silu_ready, 1)
                        if oc in (2, 4) and (more or c == 0):
                            x_high(1 - c, oc // 2 - 1)
                n.settle()

            with act.Fori(0, NCHUNK // 2 - 1) as i:
                ffn_pair(True)
            ffn_pair(False)

        @block.vector
        def _(dve):
            n = Tally(dve)

            def own():
                nc.vector.engine_nop().then_inc(dve_self, 1)
                dve.wait_ge(dve_self, n(dve_self))

            def signal(s):
                nc.vector.engine_nop().then_inc(s, 1)

            banks = Banks()

            nc.vector.memset(ones3[:, :], 1.0)
            dve.wait_ge(bias_in, 16 * 2)
            nc.vector.tensor_copy(bias_cut[:, 0, :], bias_row[:, :])
            own()
            nc.vector.tensor_tensor(bias_rest[:, :], bias_row[:, :], bias_cut[:, 0, :], ALU.subtract)
            own()
            nc.vector.tensor_copy(bias_cut[:, 1, :], bias_rest[:, :])
            own()
            nc.vector.tensor_tensor(bias_cut[:, 2, :], bias_rest[:, :], bias_cut[:, 1, :],
                                    ALU.subtract).then_inc(bias_cut_ready, 1)

            def row_stats(rows):
                for t, row in enumerate(rows):
                    nc.vector.bn_stats(stats[:, t, :], row)
                own()
                for t in range(len(rows)):
                    nc.vector.bn_aggr(mv[:, t, :], stats[:, t, :])
                own()
                nc.vector.tensor_scalar(var[:, 0:len(rows)], mv[:, 0:len(rows), 1], 1e-5, None, ALU.add).then_inc(var_ready, 1)

            def normed(to, row, t):
                return nc.vector.tensor_scalar(to, row, mv[:, t, 0:1], rstd[:, t:t + 1], ALU.subtract, ALU.mult)

            def batch_stats():
                dve.wait_ge(x_in, n(x_in, 16))
                row_stats([xin[:, t, :] for t in range(RT)])

            def norm_tile(t):
                if t == 0:
                    dve.wait_ge(rstd_ready, n(rstd_ready))
                dve.wait_ge(xn_free, n(xn_free))
                normed(xn[:, t % 2, :], xin[:, t, :], t).then_inc(xn_ready, 1)
                if t == RT - 1:
                    signal(xin_used)

            def qk_norm(t):
                dve.wait_ge(rs_ready, n(rs_ready))
                for i in range(2):
                    last = nc.vector.scalar_tensor_tensor(
                        out=qkn[:, i * D:(i + 1) * D], in0=qkraw[:, t % 2, i * D:(i + 1) * D],
                        scalar=rs[:, t % 2, i:i + 1], in1=lnw[:, i * D:(i + 1) * D], op0=ALU.mult, op1=ALU.mult)
                last.then_inc(qkn_ready, 1)

            def t_part(t):
                dve.wait_ge(rest_free, n(rest_free))
                dve.wait_ge(p1_ready, n(p1_ready))
                k, m = banks.of("T", t)
                nc.vector.tensor_tensor(rest[:, t % 2, :].rearrange("p (a r) -> p a r", a=4),
                                        m.rearrange("p (a r) -> p a r", a=4),
                                        parts[:, 0, :, t * P:(t + 1) * P], ALU.subtract).then_inc(bank_free[k], 1)
                signal(r1_ready)
                if t + 1 < RT:
                    qk_norm(t + 1)

            def fill_part(group, f):
                k, m = banks.of("fill", group, f)
                dve.wait_ge(fill_ready, n(fill_ready))
                h, pieces = f // len(FILLS), FILLS[f % len(FILLS)]
                for qt, k0, w, col, diag in pieces:
                    src = m[:, col:col + w]
                    at = slice(h * RT + qt, h * RT + qt + 1)
                    if diag:
                        last = nc.vector.tensor_tensor_reduce(
                            out=maxj[:, k, col:col + w], in0=src, in1=causal[:, BANK - w:], scale=1.0, scalar=LEAST,
                            op0=ALU.add, op1=ALU.max, accum_out=mdiag[:, at])
                    else:
                        last = nc.vector.reduce_max(mfull[:, at], src, AX_X)
                last.then_inc(bank_free[k], 1)

            def cut_maxima():
                own()
                nc.vector.tensor_tensor(mrow[:, :], mdiag[:, :], mfull[:, :], ALU.max)
                own()
                nc.vector.tensor_scalar(mrest[:, 0, :], mrow[:, :], -1.0, None, ALU.mult)
                own()
                nc.vector.tensor_copy(mcut[:, 0, :], mrest[:, 0, :])
                own()
                nc.vector.tensor_tensor(mrest[:, 1, :], mrest[:, 0, :], mcut[:, 0, :], ALU.subtract)
                own()
                nc.vector.tensor_copy(mcut[:, 1, :], mrest[:, 1, :])
                own()
                nc.vector.tensor_tensor(mcut[:, 2, :], mrest[:, 1, :], mcut[:, 1, :],
                                        ALU.subtract).then_inc(mcut_ready, 1)

            def n_part(group):
                dve.wait_ge(misc_dve, n(misc_dve))
                k, m = banks.of("N", group)
                nc.vector.tensor_copy(mcutT[0:96, :], m[0:96, 0:P // 2].bitcast(BF16)).then_inc(bank_free[k], 1)
                signal(mcutT_ready)

            dve.sem_inc(xn_free, 2)
            dve.sem_inc(rest_free, 2)
            batch_stats()
            norm_tile(0)
            norm_tile(1)
            dve.wait_ge(consts_in, 16 * 3)
            nc.vector.tensor_scalar(lnw[:, 0:D], lnw[:, 0:D], float(D ** 0.5) / float(HD ** 0.5), None, ALU.mult)
            nc.vector.tensor_scalar(lnw[:, D:], lnw[:, D:], float(D ** 0.5), None, ALU.mult)
            own()
            for kind, t in ORDER:
                if kind == "X" and 0 < t < RT - 1:
                    norm_tile(t + 1)
                if (kind, t) == ("QK", 0):
                    qk_norm(0)
                if kind == "T":
                    t_part(t)
                else:
                    banks.of(kind, t)
            n.settle()
            nc.vector.memset(mfull[:, :], LEAST)
            for g in range(NG):
                nc.vector.memset(ks[g][KROWS:SROWS, :, :].rearrange("p h s -> p (h s)").bitcast(F32), TWO_ONES)
            for c in [k * OCP for k in range(2 * KD)]:
                nc.vector.memset(idxT[:, c + INTER:c + OCP], -1.0)
            nc.vector.memset(idxT[:, DOWN0 + (OC - 1) * D:], -1.0)
            own()
            IDX = []
            for src_col in (0, UP0):
                for oc in range(OC):
                    rows = P if oc < OC - 1 else LAST
                    IDX.append((rows, [(src_col + k * OCP + oc * P, rows, P, k) for k in range(KD)]))
            for hb in range(KD):
                IDX.append((P, [(DOWN0 + oc * D + hb * P, P, P if oc < OC - 1 else LAST, oc) for oc in range(OC)]))
            seq = 0
            for m, (rows, blocks) in enumerate(IDX):
                wide = INTER if m >= 2 * OC else D
                dve.wait_ge(idx_in[m % 2], n(idx_in[m % 2], 16))
                nc.vector.tensor_copy(idx_bf[0:rows, 0:wide], idx_i[0:rows, m % 2, 0:wide]).then_inc(idx_cast, 1)
                if m + 2 < len(IDX):
                    signal(idx_used)
                for col, cols, prt, k in blocks:
                    seq += 1
                    dve.wait_ge(idx_bank, seq)
                    last = nc.vector.tensor_copy(idxT[0:prt, col:col + cols],
                                                 PROLOGUE[seq % 2][0:prt, 0:cols // 2].bitcast(BF16))
                    last.then_inc(idx_bank_free, 1)
            banks.turns = START_TURNS
            for f in range(NF):
                fill_part(0, f)
            cut_maxima()
            n_part(0)
            for f in EARLY:
                fill_part(1, f)
            dve.sem_inc(picked_free, 2)
            for i in range(2):
                dve.sem_inc(x2_stored[i], 16)
            n.settle()

            def body(b, nxt):
                jobs = place_jobs(nxt)
                banks.turns = BODY_TURNS[nxt]
                step = 0

                def job_part(job):
                    kind = job[0]
                    if kind == "T":
                        t_part(job[1])
                    elif kind == "N":
                        n_part(job[1])
                    elif kind == "C":
                        _, g, qc = job
                        dve.wait_ge(misc_dve, n(misc_dve))
                        k, m = banks.of(*job)
                        o = m[:, 0:2 * P].rearrange("p (t h c) -> p t h c", t=2, h=GH)
                        nc.vector.reciprocal(rden[:, qc % 2, :, :], o[:, :, :, HD])
                        own()
                        nc.vector.tensor_tensor(
                            attn[:, 2 * qc:2 * qc + 2, g * GH * HD:(g + 1) * GH * HD].rearrange("p t (h c) -> p t h c", h=GH),
                            o[:, :, :, 0:HD], rden[:, qc % 2, :, :].unsqueeze(3).broadcast_to([P, 2, GH, HD]),
                            ALU.mult).then_inc(bank_free[k], 1)
                    elif kind == "OP":
                        t = job[1]
                        dve.wait_ge(x2_stored[t % 2], n(x2_stored[t % 2], 16))
                        dve.wait_ge(xres_in[t % 2], n(xres_in[t % 2], 16))
                        dve.wait_ge(misc_dve, n(misc_dve))
                        k, m = banks.of(*job)
                        nc.vector.tensor_tensor(x2t[:, t % 2, :], m[:, 0:D], xres[:, t % 2, :],
                                                ALU.add).then_inc(bank_free[k], 1)
                        signal(x2_ready)

                for u in range(NG * NU):
                    g, l = divmod(u, NU)
                    for job in jobs[u - 1] if u else []:
                        job_part(job)
                    for job in jobs[u - 2] if u >= 2 else []:
                        if job == ("QK", 0):
                            qk_norm(0)
                    for group, f in fills_of(u, nxt):
                        fill_part(group, f)
                    if l == CUT_UNIT and (nxt or g < NG - 1):
                        cut_maxima()
                    if nxt and u == STATS_UNIT:
                        batch_stats()
                    for job in jobs.get(u + 1, []):
                        if job[0] == "X":
                            norm_tile(job[1])
                    if nxt and l in LUT_UNITS:
                        i, j = step % LUTB, step // LUTB
                        dve.wait_ge(picked_free, n(picked_free))
                        nc.vector.tensor_scalar(picked[:, step % 2, :], idxT[:, bass.ds((b * LUTB + i) * BANK, BANK)],
                                                float(j), lut_sb[:, j:j + 1], ALU.is_equal,
                                                ALU.mult).then_inc(picked_ready, 1)
                        step += 1
                for job in jobs[NG * NU - 1] + TAIL:
                    job_part(job)
                n.settle()

            with dve.Fori(0, B - 1) as b:
                body(b, True)
            body(B - 1, False)

            for i in range(2):
                dve.wait_ge(x2_stored[i], n(x2_stored[i], 16))
            dve.wait_ge(lut_done, 1)
            signal(stacks_read)
            signal(f_x2_used)
            signal(f_x2_used)

            def chunk_stats(c):
                dve.wait_ge(f_x2_in[c], n(f_x2_in[c], 16))
                row_stats([x2f[:, c, t, :] for t in range(TC)])

            def norm_rows(c):
                dve.wait_ge(rstd_ready, n(rstd_ready))
                for t in range(TC):
                    normed(xnf[:, t, :], x2f[:, c, t, :], t).then_inc(f_xn_ready, 1)

            def x_low(c, p):
                dve.wait_ge(f_xhi_ready, n(f_xhi_ready))
                cols = slice(2 * p * P, 2 * (p + 1) * P)
                nc.vector.tensor_tensor(xTl[:, c, :, cols].rearrange("p k (t r) -> p t k r", t=2),
                                        TB[p].rearrange("p (t k r) -> p t k r", t=2, k=KD),
                                        xTh[:, c, :, cols].rearrange("p k (t r) -> p t k r", t=2).bitcast(F32),
                                        ALU.subtract).then_inc(f_xT_ready, 1)

            for i in range(2):
                dve.sem_inc(f_stored[i], 16)
            chunk_stats(0)
            norm_rows(0)
            dve.wait_ge(f_w_hi, 1)
            nc.vector.tensor_tensor(wlo[:, :], wlook[:, :], whi[:, :].bitcast(F32), ALU.subtract).then_inc(f_w_ready, 1)
            x_low(0, 0)
            x_low(0, 1)
            n.settle()

            def ffn_pair(more):
                for c in range(2):
                    ahead = more or c == 0
                    for oc in range(OC):
                        if ahead and oc == 0:
                            chunk_stats(1 - c)
                        if ahead and oc == 1:
                            norm_rows(1 - c)
                        dve.wait_ge(f_silu_ready, n(f_silu_ready))
                        nc.vector.tensor_tensor(hf[:, oc % 2, :], silu[:, oc % 2, :], UB[oc % 2], ALU.mult)
                        nc.vector.tensor_tensor(hhi[:, oc, :], silu[:, oc % 2, :], UB[oc % 2],
                                                ALU.mult).then_inc(f_gu_free, 1)
                        own()
                        nc.vector.tensor_tensor(hlo[:, oc, :], hf[:, oc % 2, :], hhi[:, oc, :].bitcast(F32),
                                                ALU.subtract).then_inc(f_h_ready, 1)
                        if ahead and oc in (2, 4):
                            x_low(1 - c, oc // 2 - 1)
                    for t in range(TC):
                        dve.wait_ge(f_stored[t % 2], n(f_stored[t % 2], 16))
                        dve.wait_ge(f_y_ready, n(f_y_ready))
                        nc.vector.tensor_tensor(yt[:, t % 2, :], YB[t % 2][:, 0:D], x2f[:, c, t, :],
                                                ALU.add).then_inc(f_y_free, 1)
                        signal(f_out_ready)
                    if more:
                        signal(f_x2_used)
                n.settle()

            with dve.Fori(0, NCHUNK // 2 - 1) as i:
                ffn_pair(True)
            ffn_pair(False)
            for i in range(2):
                dve.wait_ge(f_stored[i], n(f_stored[i], 16))

        @block.tensor
        def _(pe):
            n = Tally(pe)

            banks, reads = Banks(), {}

            def take(*use):
                k, m = banks.of(*use)
                pe.wait_ge(bank_free[k], n(bank_free[k]))
                reads[use] = k, n.count(bank_free[k]) + 1
                return m

            def evacuated(*use):
                k, count = reads[use]
                pe.wait_ge(bank_free[k], count)

            def transpose_rows(t):
                m = take("X", t)
                pe.wait_ge(xn_ready, n(xn_ready))
                for h in range(KD):
                    last = nc.tensor.transpose(m[:, h * P:(h + 1) * P], xn[:, t % 2, h * P:(h + 1) * P], ident[:, :])
                last.then_inc(misc_act, 1)

            def project(t, c0, c1, between=lambda k: None):
                m = take("QK" if c0 == 0 else "V", t)
                w = c1 - c0
                nc.tensor.matmul(m[:, 0:w], ones3[:, :], bias[:, c0:c1], start=True, stop=False)
                for h in range(KD):
                    last = nc.tensor.matmul(m[:, 0:w], xnT[:, h, t * P:(t + 1) * P], wqkv[:, h, c0:c1],
                                            start=False, stop=h == KD - 1)
                    if h == 0 and c0 == 0:
                        last.then_inc(xn_free, 1)
                        between(1)
                last.then_inc(misc_act, 1)

            def qk(t, between=lambda k: None):
                evacuated("X", t)
                project(t, 0, 2 * D, between)

            def transpose_qk(t):
                m = take("T", t)
                pe.wait_ge(qkn_ready, n(qkn_ready))
                for a in range(4):
                    last = nc.tensor.transpose(m[:, a * P:(a + 1) * P], qkn[:, a * P:(a + 1) * P], ident[:, :])
                last.then_inc(misc_act, 1)

            def fill(group, f):
                m = take("fill", group, f)
                g = group % NG
                h, pieces = f // len(FILLS), FILLS[f % len(FILLS)]
                for qt, k0, w, col, _ in pieces:
                    last = nc.tensor.matmul(m[:, col:col + w], qs[g][0:KROWS, h, qt * P:(qt + 1) * P],
                                            ks[g][0:KROWS, h, k0:k0 + w], start=True, stop=True)
                last.then_inc(fill_ready, 1)

            def transpose_maxima(group):
                m = take("N", group)
                pe.wait_ge(mcut_ready, n(mcut_ready))
                nc.tensor.transpose(m[0:96, 0:P // 2].bitcast(BF16), mcut[:, :, :].rearrange("p a c -> p (a c)"),
                                    identb[:, :]).then_inc(misc_dve, 1)

            def scores(g, l, u):
                qc, kt = UNITS[l]
                w = width(l)
                q0 = (qc + 1) * QC - w
                if l == 0:
                    pe.wait_ge(shift_ready, n(shift_ready, 48))
                for h in range(GH):
                    last = nc.tensor.matmul(sc[:, u % 2, h, 0:w], ks[g][0:SROWS, h, kt * P:(kt + 1) * P],
                                            qs[g][0:SROWS, h, q0:q0 + w], start=True, stop=True)
                last.then_inc(sc_ready, 1)

            for k in range(4):
                pe.sem_inc(bank_free[k], 1)

            pe.wait_ge(made, 1)
            pe.wait_ge(weights_in, 16 * 2)
            pe.wait_ge(bias_placed, 48)
            for kind, t in ORDER:
                {"X": transpose_rows, "QK": qk, "T": transpose_qk}[kind](t)
            for t in (RT - 2, RT - 1):
                evacuated("T", t)
            n.settle()
            seq = 0
            for m in range(2 * OC + KD):
                pe.wait_ge(idx_cast, m + 1)
                blocks = KD if m < 2 * OC else OC
                rows = LAST if m < 2 * OC and m % OC == OC - 1 else P
                for kb in range(blocks):
                    cols = LAST if m >= 2 * OC and kb == OC - 1 else P
                    if seq >= 2:
                        pe.wait_ge(idx_bank_free, seq - 1)
                    seq += 1
                    nc.tensor.transpose(PROLOGUE[seq % 2][0:cols, 0:rows // 2].bitcast(BF16),
                                        idx_bf[0:rows, kb * P:kb * P + cols], identb[0:rows, 0:rows]).then_inc(idx_bank, 1)
            pe.wait_ge(idx_bank_free, seq)
            pe.wait_ge(stack_ready[0], n(stack_ready[0], 2 * NTERM * 16))
            banks.turns = START_TURNS
            for f in range(NF):
                fill(0, f)
            transpose_maxima(0)
            for t in range(EARLY_V):
                project(t, 2 * D, 3 * D)
            pe.wait_ge(stack_ready[1], n(stack_ready[1], 2 * NTERM * 16))
            for f in EARLY:
                fill(1, f)
            evacuated("V", EARLY_V - 1)
            scores(0, 0, 0)
            scores(0, 1, 1)
            n.settle()

            def body(b, nxt):
                jobs = place_jobs(nxt)
                banks.turns = BODY_TURNS[nxt]
                total = NG * NU

                def job_part(job, between=lambda k: None):
                    kind = job[0]
                    if kind == "V":
                        project(job[1], 2 * D, 3 * D)
                    elif kind == "X":
                        transpose_rows(job[1])
                    elif kind == "QK":
                        qk(job[1], between)
                    elif kind == "T":
                        if job[1] == 0:
                            pe.wait_ge(stack_ready[NG - 1], n(stack_ready[NG - 1], 2 * NTERM * 16))
                        transpose_qk(job[1])
                    elif kind == "N":
                        transpose_maxima(job[1])
                    elif kind == "C":
                        _, g, qc = job
                        m = take(*job)
                        for i in range(2):
                            last = nc.tensor.transpose(m[:, i * P:(i + 1) * P],
                                                       oT[:, (g * NQC + qc) % 2, i * P:(i + 1) * P], ident[:, :])
                        last.then_inc(misc_dve, 1)
                    elif kind == "OT":
                        evacuated("C", NG - 1, job[1])
                        m = take(*job)
                        for i in range(2):
                            for k in range(KD):
                                last = nc.tensor.transpose(m[:, (i * KD + k) * P:(i * KD + k + 1) * P],
                                                           attn[:, 2 * job[1] + i, k * P:(k + 1) * P], ident[:, :])
                        last.then_inc(misc_act, 1)
                    elif kind == "OP":
                        evacuated("OT", job[1] // 2)
                        m = take(*job)
                        nc.tensor.matmul(m[:, 0:D], ones3[:, :], bias[:, 3 * D:], start=True, stop=False)
                        for k in range(KD):
                            last = nc.tensor.matmul(m[:, 0:D], attnT[:, job[1] % 2, k, :], wout[:, k, :],
                                                    start=False, stop=k == KD - 1)
                        last.then_inc(misc_dve, 1)

                for u in range(total):
                    g, l = divmod(u, NU)
                    fills = fills_of(u, nxt)

                    def some_fills(k):
                        for _ in range(min(k, len(fills))):
                            group, f = fills.pop(0)
                            if f == 0 and group != NG - 1 or (group, f) == (NG - 1, 0) and not nxt:
                                pe.wait_ge(stack_ready[group % NG], n(stack_ready[group % NG], 2 * NTERM * 16))
                            fill(group, f)

                    some_fills(1)
                    pe.wait_ge(exp_done, n(exp_done))
                    if is_diag(l):
                        pe.sem_inc(exp_diag, 1)
                    if u + 2 < total:
                        scores((u + 2) // NU, (u + 2) % NU, u + 2)
                    elif nxt:
                        scores(0, (u + 2) % NU, u + 2)
                    for job in jobs[u]:
                        job_part(job, some_fills)
                    some_fills(1)
                    if g == 0 and is_diag(l) and UNITS[l][1] >= EARLY_V:
                        evacuated("V", UNITS[l][1])
                    if is_diag(l):
                        pe.wait_ge(masked, n(masked))
                    qc, kt = UNITS[l]
                    if kt == 0 and u > 0:
                        pe.wait_ge(oT_ready, n(oT_ready))
                    w = width(l)
                    for h in range(GH):
                        last = nc.tensor.matmul(ov[32 * h:32 * (h + 1), QC - w:QC],
                                                vaug[:, kt, g * GH + h, :], probs[:, u % 2, h, 0:w],
                                                start=kt == 0, stop=kt == 2 * qc + 1)
                        if h == 0 and l == NU - 3:
                            last.then_inc(stack_free, 1)
                    last.then_inc(av_done, 1)
                    some_fills(len(fills))
                pe.wait_ge(oT_ready, n(oT_ready))
                for job in TAIL:
                    job_part(job)
                if nxt:
                    evacuated("V", EARLY_V - 1)
                n.settle()

            with pe.Fori(0, B - 1) as b:
                body(b, True)
            body(B - 1, False)

            for k in range(NRING):
                pe.wait_ge(bank_free[k], 1)

            def transpose_pair(c, p):
                for i in range(2):
                    t = 2 * p + i
                    pe.wait_ge(f_xn_ready, n(f_xn_ready))
                    for k in range(KD):
                        last = nc.tensor.transpose(TB[p][:, (i * KD + k) * P:(i * KD + k + 1) * P],
                                                   xnf[:, t, k * P:(k + 1) * P], ident[:, :])
                last.then_inc(f_tr_ready, 1)

            transpose_pair(0, 0)
            transpose_pair(0, 1)
            pe.wait_ge(f_w_ready, 1)
            pe.wait_ge(f_xT_ready, n(f_xT_ready, 2))
            pe.sem_inc(f_gu_free, 2)
            pe.sem_inc(f_y_free, 2)
            n.settle()

            def weight(at, width, high):
                return (whi if high else wlo)[:, at:at + width]

            def ffn_pair(more):
                for c in range(2):
                    ahead = more or c == 0
                    for oc in range(OC):
                        pe.wait_ge(f_gu_free, n(f_gu_free))
                        for col0, dst in ((0, GB[oc % 2]), (UP0, UB[oc % 2])):
                            terms = [(k, wh, xh) for k in range(KD) for wh, xh in ((1, 1), (0, 1), (1, 0))]
                            for i, (k, wh, xh) in enumerate(terms):
                                last = nc.tensor.matmul(dst, weight(col0 + k * OCP + oc * P, P, wh), (xTh if xh else xTl)[:, c, k, :],
                                                        start=i == 0, stop=i == len(terms) - 1)
                        last.then_inc(f_gu_ready, 1)
                        if ahead and oc in (1, 3):
                            transpose_pair(1 - c, oc // 2)
                    for p in range(TC // 2):
                        for pieces in (range(OC - 1), range(OC - 1, OC)):
                            for i in range(2):
                                t = 2 * p + i
                                if 0 in pieces:
                                    pe.wait_ge(f_y_free, n(f_y_free))
                                for oc in pieces:
                                    if t == 0:
                                        pe.wait_ge(f_h_ready, n(f_h_ready))
                                    for j, (hh, wh) in enumerate(((1, 1), (0, 1), (1, 0))):
                                        last = nc.tensor.matmul(YB[i][:, 0:D], (hhi if hh else hlo)[:, oc, t * P:(t + 1) * P],
                                                                weight(DOWN0 + oc * D, D, wh), start=oc == 0 and j == 0,
                                                                stop=oc == OC - 1 and j == 2)
                                if OC - 1 in pieces:
                                    last.then_inc(f_y_ready, 1)
                    if ahead:
                        pe.wait_ge(f_xT_ready, n(f_xT_ready, 2))
                n.settle()

            with pe.Fori(0, NCHUNK // 2 - 1) as i:
                ffn_pair(True)
            ffn_pair(False)


_INS = ['L0_attn_x', 'L0_attn_w_qkv', 'L0_attn_b_qkv', 'L0_attn_q_ln_w', 'L0_attn_k_ln_w', 'L0_attn_w_out',
        'L0_attn_b_out', 'L0_ffn_lut', 'L0_ffn_gate_idx', 'L0_ffn_up_idx', 'L0_ffn_down_idx']


def kernel(**inputs):
    import numpy as _np
    import concourse.bacc as _bacc
    from concourse import mybir as _mybir
    from concourse.bass_utils import run_bass_kernel_spmd as _run

    nc = _bacc.Bacc("TRN2", target_bir_lowering=False, num_devices=1)
    arrays, args = {}, []
    for name in _INS:
        a = _np.ascontiguousarray(inputs[name])
        arrays[f"in_{name}_dram"] = a
        args.append(nc.dram_tensor(f"in_{name}_dram", a.shape, _mybir.dt.from_np(a.dtype), kind="ExternalInput").ap())
    shape = inputs['L0_attn_x'].shape
    args.append(nc.dram_tensor("out_0_dram", shape, _mybir.dt.float32, kind="ExternalOutput").ap())
    layer_kernel(nc, *args)
    r = _run(nc, [arrays], core_ids=[0])
    return r.results[0]["out_0_dram"]
```

```python
import struct
from contextlib import ExitStack

import concourse.bass as bass
from concourse import mybir

F32 = mybir.dt.float32
F32R = mybir.dt.float32r
BF16 = mybir.dt.bfloat16
I32 = mybir.dt.int32
ALU = mybir.AluOpType
ACT = mybir.ActivationFunctionType
AX_X = mybir.AxisListType.X

P = 128
BANK = 512
MASKED = -1.0e30
LEAST = -3.0e38
TWO_ONES = struct.unpack("<f", struct.pack("<I", 0x3F803F80))[0]


class Tally:

    def __init__(self, eng):
        self.eng, self.seen = eng, {}

    def __call__(self, sem, by=1):
        name = sem.name
        self.seen[name] = (sem, self.seen.get(name, (sem, 0))[1] + by)
        return self.seen[name][1]

    def count(self, sem):
        return self.seen.get(sem.name, (sem, 0))[1]

    def settle(self):
        self.eng.drain()
        for sem, n in self.seen.values():
            self.eng.sem_inc(sem, -n)
        self.seen = {}


def layer_kernel(nc, x, w_qkv, b_qkv, q_ln_w, k_ln_w, w_out, b_out, lut, gate_idx, up_idx, down_idx, out):
    B, S, D = x.shape
    H = 16
    HD = D // H
    INTER = gate_idx.shape[0]
    NLUT = lut.shape[0]
    KD = D // P
    RT = S // P
    GH = 4
    NG = H // GH
    QC = 256
    NQC = S // QC
    NTERM = 6
    Q_PART = [0, 0, 0, 1, 1, 2]
    K_PART = [0, 1, 2, 0, 1, 0]
    KROWS = NTERM * HD
    SROWS = KROWS + 3
    OC = (INTER + P - 1) // P
    OCP = OC * P
    LAST = INTER - (OC - 1) * P
    WCOLS = 2 * KD * OCP + OC * D
    UP0, DOWN0 = KD * OCP, 2 * KD * OCP
    NCH = WCOLS // BANK
    LUTB = NCH // (B - 1)
    assert S == 4 * D and NCH % (B - 1) == 0 and RT == 8 and KD == 2 and D == 256
    CH = 512
    NCHUNK = B * S // CH
    STATS_AT = {OC - 4: (0,), OC - 3: (1,), OC - 2: (2, 3)}
    TC = CH // P

    UNITS = [(qc, kt) for qc in range(NQC) for kt in range(2 * qc + 2)]
    NU = len(UNITS)
    CHUNK_END = {UNITS.index((qc, 2 * qc + 1)): qc for qc in range(NQC)}

    def is_diag(l):
        qc, kt = UNITS[l]
        return kt >= 2 * qc

    def width(l):
        qc, kt = UNITS[l]
        return P if kt == 2 * qc + 1 else QC

    FILLS = [
        [(4, 0, 512, 0, False)],
        [(5, 0, 512, 0, False)],
        [(6, 0, 512, 0, False)],
        [(7, 0, 512, 0, False)],
        [(0, 0, 128, 0, True), (2, 0, 384, 128, True)],
        [(3, 0, 512, 0, True)],
        [(4, 512, 128, 0, True), (6, 512, 384, 128, True)],
        [(7, 512, 512, 0, True)],
        [(1, 0, 256, 0, True), (5, 512, 256, 256, True)],
    ]
    NF = len(FILLS) * GH
    FILL_LEAD = 6

    def fill_unit(group, f):
        return NU * (group - 1) - FILL_LEAD + f * NU // NF

    def fills_of(u, nxt):
        groups = range(1, NG + 2 if nxt else NG)
        return [(g, f) for g in groups for f in range(NF) if fill_unit(g, f) == u]

    EARLY = [f for f in range(NF) if fill_unit(1, f) < 0]
    CUT_UNIT = NU - FILL_LEAD - 1

    STEPS = []
    for t in range(RT):
        STEPS.append([("X", t)] + ([("T", t - 2)] if t >= 2 else []))
        STEPS.append([("Q", t)] + ([("R", t - 1)] if t >= 1 else []))
        STEPS.append([("K", t)])
    STEPS += [[("T", RT - 2)], [("R", RT - 1)], [], [("T", RT - 1)]]
    STATS_UNITS = [2, 3, 4, 5]
    EARLY_V = 2

    LUT_UNITS = [l for l in range(NU) if not is_diag((l + 1) % NU)]
    assert len(LUT_UNITS) * NG == NLUT * LUTB

    TAIL = [("C", NG - 1, NQC - 1), ("OT", 3), ("OP", 6), ("OP", 7)]

    def place_jobs(carry, nxt):
        jobs = {u: [] for u in range(NG * NU)}
        if carry:
            for u, job in zip([0, 2, 3, 5], TAIL, strict=True):
                jobs[u].append(job + ("before",))
        for g in range(NG):
            for l, qc in CHUNK_END.items():
                u = NU * g + l + (4 if qc == NQC - 2 else 3)
                if u < NG * NU:
                    jobs[u].append(("C", g, qc))
            if g < NG - 1 or nxt:
                jobs[NU * g + CUT_UNIT + 1].append(("N", (g + 1) % NG))
        if nxt:
            free = [u for u in range(STATS_UNITS[-1] + 2, 3 * NU - FILL_LEAD - 7) if not jobs[u]]
            for u, step in zip(free, STEPS, strict=False):
                jobs[u] += step
            assert len(free) >= len(STEPS)
        for t, u in zip(range(EARLY_V, RT), [1, 3, 6, 8, 14, 15], strict=True):
            jobs[u].append(("V", t))
        g0 = (NG - 1) * NU
        for u, job in [(5, ("OT", 0)), (6, ("OP", 0)), (7, ("OP", 1)), (9, ("OT", 1)), (10, ("OP", 2)),
                       (11, ("OP", 3)), (16, ("OT", 2)), (17, ("OP", 4)), (18, ("OP", 5))]:
            jobs[g0 + u].append(job)
        if nxt:
            jobs[g0 + 13].append(("V", 0))
            jobs[g0 + 19].append(("V", 1))
        else:
            for u, job in [(-6, ("S", 0)), (-3, ("FN", 0)), (0, ("FT", 0)), (1, ("FT", 1))]:
                jobs[g0 + u].append(job)
            for i in range(NCH):
                jobs[g0 - FILL_LEAD + i].append(("W", i))
        return jobs

    NO_BANK = ("R", "S", "FN", "W")
    NRING = 3

    def turns(uses):
        return {use: i % NRING for i, use in enumerate(uses)}

    def unit_uses(u, carry, nxt):
        fills = [("fill", g, f) for g, f in fills_of(u, nxt)]
        return fills[:1] + [job for job in place_jobs(carry, nxt)[u] if job[0] not in NO_BANK] + fills[1:]

    START_TURNS = turns([("fill", 0, f) for f in range(NF)] + [("N", 0)] + [("V", t) for t in range(EARLY_V)]
                        + [("fill", 1, f) for f in EARLY])
    BODY_TURNS = {(carry, nxt): turns([use for u in range(NG * NU) for use in unit_uses(u, carry, nxt)] + TAIL)
                  for carry, nxt in ((False, True), (True, True), (True, False))}

    with ExitStack() as ctx:
        def sb(name, shape, dt=F32):
            return ctx.enter_context(nc.sbuf_tensor(name, shape, dt))

        def sem(name):
            return ctx.enter_context(nc.semaphore(name))

        ident = sb("ident", [P, P])
        identb = sb("identb", [P, P], BF16)
        causal = sb("causal", [P, BANK], BF16)
        wqkv = sb("wqkv", [P, KD, 3 * D])
        wout = sb("wout", [P, KD, D])
        lnw = sb("lnw", [P, 2 * D])
        bias = sb("bias", [3, 4 * D], BF16)
        ones3 = sb("ones3", [3, P], BF16)
        lut_sb = sb("lut_sb", [P, NLUT])
        xin = sb("xin", [P, RT, D])
        xn = sb("xn", [P, 2, D])
        xnT = sb("xnT", [P, KD, S])
        stats = sb("stats", [P, RT, 6])
        mv = sb("mv", [P, RT, 2])
        var = sb("var", [P, RT])
        rstd = sb("rstd", [P, RT])
        minus_half = sb("minus_half", [P, RT])
        ss = sb("ss", [P, 2, 2])
        sse = sb("sse", [P, 2, 2])
        rs = sb("rs", [P, 2, 2])
        probs = sb("probs", [P, 2, GH, QC])
        maxj = sb("maxj", [P, NRING, BANK], BF16)
        mdiag = sb("mdiag", [P, GH * RT])
        mfull = sb("mfull", [P, GH * RT])
        mrow = sb("mrow", [P, GH * RT])
        mrest = sb("mrest", [P, 2, GH * RT])
        mcut = sb("mcut", [P, 3, GH * RT], BF16)
        mcutT = sb("mcutT", [P, P], BF16)
        oT = sb("oT", [P, 2, QC])
        rden = sb("rden", [P, 2, 2, GH])
        attn = sb("attn", [P, RT, D])
        attnT = sb("attnT", [P, 2, KD, P])
        xres = sb("xres", [P, 2, D])
        x2t = sb("x2t", [P, 2, D])
        idxT = sb("idxT", [P, WCOLS], BF16)
        wlook = sb("wlook", [P, WCOLS])
        picked = sb("picked", [P, 2, BANK])
        with ExitStack() as attention:
            def sba(name, shape, dt=F32):
                return attention.enter_context(nc.sbuf_tensor(name, shape, dt))

            sqj = sba("sqj", [P, 2, D], BF16)
            qkraw = sba("qkraw", [P, 2, 2 * D])
            qkn = sba("qkn", [P, 2 * D])
            parts = sba("parts", [P, 3, 4, S], BF16)
            rest = sba("rest", [P, 2, BANK])
            qs = [sba(f"qs{g}", [P, GH, S], BF16) for g in range(NG)]
            ks = [sba(f"ks{g}", [P, GH, S], BF16) for g in range(NG)]
            vaug = sba("vaug", [P, RT, H, 32])
        whi = sb("whi", [P, WCOLS], F32R)
        wlo = sb("wlo", [P, WCOLS], F32R)
        xTh = sb("xTh", [P, 2, KD, CH], F32R)
        xTl = sb("xTl", [P, 2, KD, CH], F32R)
        hhi = sb("hhi", [P, OC, CH], F32R)
        hlo = sb("hlo", [P, OC, CH], F32R)
        parts_dram = nc.dram_tensor("parts_scratch", (3, 4, P, S), BF16, kind="Internal").ap()
        x2_dram = nc.dram_tensor("x2_scratch", (B * S, D), F32, kind="Internal").ap()

        sc = ctx.enter_context(nc.psum_tensor("sc", [P, 2, GH, QC], F32))
        mx = ctx.enter_context(nc.psum_tensor("mx", [P, 2, BANK], F32))
        ov = ctx.enter_context(nc.psum_tensor("ov", [P, BANK], F32))
        ms = ctx.enter_context(nc.psum_tensor("ms", [P, BANK], F32))
        scf = sc[:].rearrange("p a h q -> p (a h q)")
        PROLOGUE = [ms[:, :]] + [scf[:, BANK * i:BANK * (i + 1)] for i in range(3)]
        RING = [ms[:, :], mx[:, 0, :], mx[:, 1, :]]

        class Banks:

            def __init__(self):
                self.turn, self.turns = 0, None

            def of(self, *use):
                if self.turns is None:
                    k = self.turn % len(PROLOGUE)
                    self.turn += 1
                    return k, PROLOGUE[k]
                k = self.turns[use]
                return k, RING[k]

        bias_in, consts_in, x_in = sem("bias_in"), sem("consts_in"), sem("x_in")
        weights_in, wout_in = sem("weights_in"), sem("wout_in")
        bias_cut_ready, bias_placed, made = sem("bias_cut_ready"), sem("bias_placed"), sem("made")
        vaug_made = sem("vaug_made")
        idx_in, idx_read = sem("idx_in"), sem("idx_read")
        idx_cast, idx_bank, idx_bank_free = sem("idx_cast"), sem("idx_bank"), sem("idx_bank_free")
        xin_used = sem("xin_used")
        xn_ready, xn_free = sem("xn_ready"), sem("xn_free")
        bank_free = [sem(f"bank_free{i}") for i in range(4)]
        misc_act, misc_dve = sem("misc_act"), sem("misc_dve")
        var_ready, rstd_ready = sem("var_ready"), sem("rstd_ready")
        ss_ready, rs_ready, qkn_ready = sem("ss_ready"), sem("rs_ready"), sem("qkn_ready")
        p1_ready, r1_ready, p2_ready, rest_free = sem("p1_ready"), sem("r1_ready"), sem("p2_ready"), sem("rest_free")
        parts_ready, parts_stored = sem("parts_ready"), sem("parts_stored")
        stack_ready = [sem(f"stack_ready{g}") for g in range(NG)]
        stack_free = sem("stack_free")
        fill_ready = sem("fill_ready")
        mcut_ready, mcutT_ready = sem("mcut_ready"), sem("mcutT_ready")
        shift_ready = sem("shift_ready")
        sc_ready = sem("sc_ready")
        exp_done, exp_diag, masked = sem("exp_done"), sem("exp_diag"), sem("masked")
        av_done, oT_ready = sem("av_done"), sem("oT_ready")
        xres_in = [sem("xres_in0"), sem("xres_in1")]
        x2_ready = sem("x2_ready")
        x2_stored = [sem("x2_stored0"), sem("x2_stored1")]
        picked_ready, picked_free, lut_done = sem("picked_ready"), sem("picked_free"), sem("lut_done")
        dve_self, pool_self = sem("dve_self"), sem("pool_self")
        f_x2_in = [sem("f_x2_in0"), sem("f_x2_in1")]
        f_x2_used = sem("f_x2_used")
        f_w_hi = sem("f_w_hi")
        f_xn_ready = sem("f_xn_ready")
        f_tr_ready, f_xhi_ready, f_xT_ready = sem("f_tr_ready"), sem("f_xhi_ready"), sem("f_xT_ready")
        f_gu_ready, f_silu_ready, f_gu_free, f_h_ready = sem("f_gu_ready"), sem("f_silu_ready"), sem("f_gu_free"), sem("f_h_ready")
        f_y_ready, f_y_free, f_out_ready = sem("f_y_ready"), sem("f_y_free"), sem("f_out_ready")
        f_stored = [sem("f_stored0"), sem("f_stored1")]

        x_rows = x.rearrange("b (t p) d -> b p t d", p=P)
        x_flat = x.rearrange("b s d -> (b s) d")
        out_flat = out.rearrange("b s d -> (b s) d")

        x2f = xin[:, :, :].rearrange("p (c t) d -> p c t d", c=2)
        silu = probs[:, :, :, :].rearrange("p a h q -> p a (h q)")[:, :, 0:CH]
        hf = xnT[:, :, 0:CH]
        yt = x2t
        xnf = [xnT[:, t // 2, S // 2 + t % 2 * D:S // 2 + (t % 2 + 1) * D] for t in range(TC)]
        idx_i = wlook[:, :].bitcast(I32)
        idx_gu = idx_i[:, 0:2 * OC * D].rearrange("p (g c d) -> p g c d", g=2, c=OC)
        idx_down = idx_i[:, 2 * OC * D:2 * OC * D + KD * INTER].rearrange("p (h n) -> p h n", h=KD)
        idx_gub = probs[:, :, :, :].rearrange("p a h q -> p (a h q)").bitcast(BF16)[:, 0:2 * OC * D].rearrange("p (g c d) -> p g c d", g=2, c=OC)
        idx_downb = attn[:, :, :].rearrange("p t d -> p (t d)").bitcast(BF16)[:, 0:KD * INTER].rearrange("p (h n) -> p h n", h=KD)
        IDX_BANKS = []
        for i in range(2):
            for k in range(KD):
                IDX_BANKS.append((P, (i * KD + k) * OCP, INTER,
                                  [idx_gub[0:min(P, INTER - c * P), i, c, k * P:(k + 1) * P] for c in range(OC)]))
        for c0, c1 in ((0, 4), (4, OC - 1), (OC - 1, OC)):
            rows = min(P, INTER - c0 * P)
            IDX_BANKS.append((rows, DOWN0 + c0 * D, (c1 - c0) * D,
                              [idx_downb[:, h, c * P:c * P + rows] for c in range(c0, c1) for h in range(KD)]))

        bias_row = attn[0:3, 0:4, :].rearrange("p a d -> p (a d)")
        bias_rest = attn[0:3, 4:8, :].rearrange("p a d -> p (a d)")
        bias_cut = parts[0:3, :, 0, :]
        GB = [scf[:, 0:BANK], scf[:, BANK:2 * BANK]]
        UB = [scf[:, 2 * BANK:3 * BANK], scf[:, 3 * BANK:4 * BANK]]
        YB = [mx[:, 0, :], mx[:, 1, :]]
        TB = [ov[:, :], ms[:, :]]

        block = ctx.enter_context(nc.Block())

        @block.sync
        def _(sp):
            n = Tally(sp)
            sp.dma_start(xin[:, :, :], x_rows[0]).then_inc(x_in, 16)
            sp.dma_start(bias_row[:, 0:3 * D], b_qkv.partition_broadcast(3)).then_inc(bias_in, 16)
            sp.dma_start(bias_row[:, 3 * D:], b_out.partition_broadcast(3)).then_inc(bias_in, 16)
            sp.dma_start(wqkv[:, :, :], w_qkv.rearrange("(k p) n -> p k n", p=P)).then_inc(weights_in, 16)
            sp.dma_start(lnw[:, 0:D], q_ln_w.partition_broadcast(P)).then_inc(consts_in, 16)
            sp.dma_start(lnw[:, D:], k_ln_w.partition_broadcast(P)).then_inc(consts_in, 16)
            sp.wait_ge(bias_cut_ready, 1)
            for i in range(3):
                sp.dma_start(bias[i:i + 1, :], bias_cut[i:i + 1, i, :]).then_inc(bias_placed, 16)
            sp.dma_start(wout[:, :, :], w_out.rearrange("(k p) n -> p k n", p=P)).then_inc(wout_in, 16)
            sp.dma_start(lut_sb[:, :], lut.partition_broadcast(P)).then_inc(consts_in, 16)

            def parts_out(quarters):
                for i in quarters:
                    sp.wait_ge(parts_ready, n(parts_ready))
                    cols = slice(i * S // 4, (i + 1) * S // 4)
                    sp.dma_start(parts_dram[:, :, :, cols].rearrange("i a p s -> p i a s"),
                                 parts[:, :, :, cols]).then_inc(parts_stored, 16)
                if 3 in quarters:
                    sp.wait_ge(parts_stored, n(parts_stored, 4 * 16))

            def stack(g):
                p0 = (g % 2) * (GH * HD)
                for dst, half, terms in ((qs[g], g // 2, Q_PART), (ks[g], 2 + g // 2, K_PART)):
                    for j, part in enumerate(terms):
                        sp.dma_start(dst[HD * j:HD * (j + 1), :, :],
                                     parts_dram[part, half, p0:p0 + GH * HD, :].rearrange("(h d) s -> d h s", h=GH)
                                     ).then_inc(stack_ready[g], 16)

            def shift(g):
                sp.wait_ge(mcutT_ready, n(mcutT_ready))
                for i in range(3):
                    sp.dma_start(qs[g][KROWS + i:KROWS + i + 1, :, :].rearrange("p h (t n) -> p (h t) n", n=P),
                                 mcutT[32 * i:32 * (i + 1), :]).then_inc(shift_ready, 16)

            def x2_out(r0, t):
                sp.wait_ge(x2_ready, n(x2_ready))
                sp.dma_start(x2_dram[bass.ds(r0 + t * P, P), :], x2t[:, t % 2, :]).then_inc(x2_stored[t % 2], 16)

            sp.sem_inc(stack_free, 1)
            parts_out(range(4))
            for g in range(NG - 1):
                stack(g)
            shift(0)

            def body(b, carry, nxt):
                if nxt:
                    sp.wait_ge(xin_used, n(xin_used))
                    sp.dma_start(xin[:, :, :], x_rows[b + 1]).then_inc(x_in, 16)
                else:
                    sp.wait_ge(xin_used, n(xin_used))
                    for c in range(2):
                        sp.dma_start(x2f[:, c], x2_dram[c * CH:(c + 1) * CH, :].rearrange("(t p) d -> p t d", p=P)
                                     ).then_inc(f_x2_in[c], 16)
                sp.wait_ge(stack_free, n(stack_free))
                stack(NG - 1)
                if carry:
                    for t in (RT - 2, RT - 1):
                        x2_out((b - 1) * S, t)
                shift(1)
                if nxt:
                    parts_out((0, 1))
                shift(2)
                if nxt:
                    sp.wait_ge(stack_free, n(stack_free))
                    parts_out((2, 3))
                    stack(0)
                shift(3)
                if nxt:
                    sp.wait_ge(stack_free, n(stack_free))
                    stack(1)
                    sp.wait_ge(stack_free, n(stack_free))
                    stack(2)
                else:
                    sp.wait_ge(stack_free, n(stack_free, NG - 1))
                r0 = b * S
                for t in range(2):
                    sp.dma_start(xres[:, t, :], x_flat[bass.ds(r0 + t * P, P), :]).then_inc(xres_in[t], 16)
                for t in range(RT - 2 if nxt else RT):
                    if t == 4 and nxt:
                        shift(0)
                    x2_out(r0, t)
                    if t + 2 < RT:
                        sp.dma_start(xres[:, t % 2, :],
                                     x_flat[bass.ds(r0 + (t + 2) * P, P), :]).then_inc(xres_in[t % 2], 16)
                n.settle()

            n.settle()
            body(0, False, True)
            with sp.Fori(1, B - 1) as b:
                body(b, True, True)
            body(B - 1, True, False)

            def ffn_pair(i, more):
                for c in range(2):
                    r0 = (2 * i + c) * CH
                    for t in range(TC):
                        sp.wait_ge(f_out_ready, n(f_out_ready))
                        sp.dma_start(out_flat[bass.ds(r0 + t * P, P), :], yt[:, t % 2, :]).then_inc(f_stored[t % 2], 16)
                    if more:
                        sp.wait_ge(f_x2_used, n(f_x2_used))
                        sp.dma_start(x2f[:, c], x2_dram[bass.ds(r0 + 2 * CH, CH), :].rearrange("(t p) d -> p t d", p=P)
                                     ).then_inc(f_x2_in[c], 16)
                n.settle()

            with sp.Fori(0, NCHUNK // 2 - 1) as i:
                ffn_pair(i, True)
            ffn_pair(NCHUNK // 2 - 1, False)

        @block.gpsimd
        def _(pool):
            n = Tally(pool)
            nc.gpsimd.memset(ident[:, :], 0.0).then_inc(pool_self, 1)
            pool.wait_ge(pool_self, 1)
            nc.gpsimd.affine_select(out=ident[:, :], in_=ident[:, :], compare_op=ALU.not_equal, fill=1.0, base=0,
                                    pattern=[[-1, P]], channel_multiplier=1).then_inc(pool_self, 1)
            pool.wait_ge(pool_self, 2)
            nc.gpsimd.tensor_copy(identb[:, :], ident[:, :])
            nc.gpsimd.memset(causal[:, :], 0.0).then_inc(pool_self, 1)
            pool.wait_ge(pool_self, 3)
            tri = causal[:, BANK - P:]
            nc.gpsimd.affine_select(out=tri, in_=tri, compare_op=ALU.is_ge, fill=MASKED, base=0,
                                    pattern=[[-1, P]], channel_multiplier=1)
            nc.gpsimd.memset(minus_half[:, :], -0.5)
            pool.drain().then_inc(made, 1)

            def last_part(t):
                pool.wait_ge(p2_ready, n(p2_ready))
                r = rest[:, t % 2, :].rearrange("p (a r) -> p a r", a=4)
                cols = slice(t * P, (t + 1) * P)
                nc.gpsimd.tensor_tensor(parts[:, 2, :, cols], r, parts[:, 1, :, cols],
                                        ALU.subtract).then_inc(rest_free, 1)
                if t % 2 == 1:
                    pool.drain().then_inc(parts_ready, 1)

            def roots_of_rows(m):
                pool.wait_ge(var_ready, n(var_ready))
                nc.gpsimd.tensor_tensor(rstd[:, 0:m], var[:, 0:m], minus_half[:, 0:m], ALU.pow).then_inc(rstd_ready, 1)

            def roots_of_qk(t):
                pool.wait_ge(ss_ready, n(ss_ready))
                nc.gpsimd.tensor_scalar(sse[:, t % 2, :], ss[:, t % 2, :], D * 1e-6, None, ALU.add).then_inc(pool_self, 1)
                pool.wait_ge(pool_self, n(pool_self))
                nc.gpsimd.tensor_tensor(rs[:, t % 2, :], sse[:, t % 2, :], minus_half[:, 0:2],
                                        ALU.pow).then_inc(rs_ready, 1)

            pool.sem_inc(pool_self, -3)
            nc.gpsimd.memset(vaug[:, :, :, :].rearrange("p t h c -> p (t h c)"), 0.0).then_inc(pool_self, 1)
            pool.wait_ge(pool_self, n(pool_self))
            nc.gpsimd.memset(vaug[:, :, :, HD:HD + 1], 1.0).then_inc(vaug_made, 1)
            roots_of_rows(RT)
            for step in STEPS:
                for kind, t in step:
                    if kind == "K":
                        roots_of_qk(t)
                    elif kind == "T":
                        last_part(t)
            pool.wait_ge(idx_read, 1)
            nc.gpsimd.memset(wlook[:, :], 0.0)
            n.settle()

            def body(b, carry, nxt):
                jobs = place_jobs(carry, nxt)
                step = 0
                for u in range(NG * NU):
                    l = u % NU
                    if is_diag(l):
                        pool.wait_ge(exp_diag, n(exp_diag))
                        p = probs[:, u % 2, :, 0:P]
                        nc.gpsimd.affine_select(out=p, in_=p, compare_op=ALU.is_ge, fill=0.0, base=0,
                                                pattern=[[0, GH], [1, P]], channel_multiplier=-1).then_inc(masked, 1)
                    for job in jobs.get(u - 2, []):
                        if job[0] == "T":
                            last_part(job[1])
                    for job in jobs.get(u - 1, []):
                        if job[0] == "K":
                            roots_of_qk(job[1])
                    if nxt and u == STATS_UNITS[-1] + 1:
                        roots_of_rows(RT)
                    if ("S", 0) in jobs.get(u - 1, []):
                        roots_of_rows(TC)
                    if nxt and l in LUT_UNITS:
                        i = step % LUTB
                        pool.wait_ge(picked_ready, n(picked_ready))
                        w = wlook[:, bass.ds((b * LUTB + i) * BANK, BANK)]
                        nc.gpsimd.tensor_tensor(w, w, picked[:, step % 2, :], ALU.add).then_inc(picked_free, 1)
                        step += 1
                n.settle()

            body(0, False, True)
            with pool.Fori(1, B - 1) as b:
                body(b, True, True)
            pool.drain().then_inc(lut_done, 1)
            body(B - 1, True, False)
            with pool.Fori(0, NCHUNK // 2 - 1) as i:
                roots_of_rows(TC)
                roots_of_rows(TC)
                n.settle()
            roots_of_rows(TC)

        @block.scalar
        def _(act):
            n = Tally(act)

            def x_part(t):
                act.wait_ge(misc_act, n(misc_act))
                k, m = banks.of("X", t)
                nc.scalar.copy(xnT[:, :, t * P:(t + 1) * P],
                               m[:, 0:D].rearrange("p (k r) -> p k r", k=KD)).then_inc(bank_free[k], 1)

            def v_part(t):
                act.wait_ge(misc_act, n(misc_act))
                k, m = banks.of("V", t)
                nc.scalar.copy(vaug[:, t, :, 0:HD],
                               m[:, 0:D].rearrange("p (h c) -> p h c", h=H)).then_inc(bank_free[k], 1)

            def qk_part(i, t):
                act.wait_ge(misc_act, n(misc_act))
                k, m = banks.of("QK"[i], t)
                nc.scalar.copy(qkraw[:, t % 2, i * D:(i + 1) * D], m[:, 0:D])
                last = nc.scalar.activation(sqj[:, i, :], m[:, 0:D], ACT.Square, accum_out=ss[:, t % 2, i:i + 1])
                if i == 0:
                    last.then_inc(bank_free[k], 1)
                else:
                    last.then_inc(ss_ready, 1)
                    act.drain().then_inc(bank_free[k], 1)

            def t_part(t):
                act.wait_ge(misc_act, n(misc_act))
                k, m = banks.of("T", t)
                nc.scalar.copy(parts[:, 0, :, t * P:(t + 1) * P],
                               m.rearrange("p (a r) -> p a r", a=4)).then_inc(p1_ready, 1)

            def second_part(t):
                act.wait_ge(r1_ready, n(r1_ready))
                nc.scalar.copy(parts[:, 1, :, t * P:(t + 1) * P],
                               rest[:, t % 2, :].rearrange("p (a r) -> p a r", a=4)).then_inc(p2_ready, 1)

            banks = Banks()

            full = (OC - 1) * P
            for i, src in enumerate((gate_idx, up_idx)):
                act.dma_start(idx_gu[:, i, 0:OC - 1, :], src[0:full, :].rearrange("(c p) d -> p c d", p=P)).then_inc(idx_in, 16)
                act.dma_start(idx_gu[0:LAST, i, OC - 1, :], src[full:, :]).then_inc(idx_in, 16)
            act.dma_start(idx_down[:, :, :], down_idx.rearrange("(h p) n -> p h n", p=P)).then_inc(idx_in, 16)
            act.wait_ge(made, 1)
            for i, step in enumerate(STEPS):
                for kind, t in step:
                    if kind == "X":
                        x_part(t)
                    elif kind in "QK":
                        qk_part("QK".index(kind), t)
                    elif kind == "T":
                        t_part(t)
                for kind, t in STEPS[i - 1] if i else []:
                    if kind == "T":
                        second_part(t)
            second_part(RT - 1)
            act.wait_ge(idx_in, 5 * 16)
            for i in range(2):
                nc.scalar.copy(idx_gub[:, i, 0:OC - 1, :], idx_gu[:, i, 0:OC - 1, :])
                nc.scalar.copy(idx_gub[0:LAST, i, OC - 1, :], idx_gu[0:LAST, i, OC - 1, :])
            nc.scalar.copy(idx_downb[:, :, :], idx_down[:, :, :]).then_inc(idx_cast, 1)
            for seq, (rows, c0, cols, _) in enumerate(IDX_BANKS):
                act.wait_ge(idx_bank, seq + 1)
                nc.scalar.copy(idxT[0:rows, c0:c0 + cols],
                               PROLOGUE[seq % 4].bitcast(BF16)[0:rows, 0:cols]).then_inc(idx_bank_free, 1)
            act.wait_ge(vaug_made, 1)
            banks.turns = START_TURNS
            for t in range(EARLY_V):
                v_part(t)
            n.settle()

            def x_high(c, p, bank):
                nc.scalar.copy(xTh[:, c, :, 2 * p * P:2 * (p + 1) * P].rearrange("p k (t r) -> p t k r", t=2),
                               bank.rearrange("p (t k r) -> p t k r", t=2, k=KD)).then_inc(f_xhi_ready, 1)

            def body(b, carry, nxt):
                jobs = place_jobs(carry, nxt)
                banks.turns = BODY_TURNS[carry, nxt]

                def out_chunk(u):
                    act.wait_ge(av_done, u + 1)
                    c = u // NU * NQC + CHUNK_END[u % NU]
                    nc.scalar.copy(oT[:, c % 2, :], ov[:, 0:QC]).then_inc(oT_ready, 1)

                def job_part(job):
                    kind = job[0]
                    if kind == "V":
                        v_part(job[1])
                    elif kind == "X":
                        x_part(job[1])
                    elif kind in "QK":
                        qk_part("QK".index(kind), job[1])
                    elif kind == "T":
                        t_part(job[1])
                    elif kind == "FT":
                        act.wait_ge(misc_act, n(misc_act))
                        x_high(0, job[1], banks.of(*job)[1])
                    elif kind == "W":
                        cols = slice(job[1] * BANK, (job[1] + 1) * BANK)
                        nc.scalar.copy(whi[:, cols], wlook[:, cols]).then_inc(f_w_hi, 1)
                    elif kind == "OT":
                        act.wait_ge(misc_act, n(misc_act))
                        k, m = banks.of(*job)
                        nc.scalar.copy(attnT[:, :, :, :].rearrange("p t k r -> p (t k r)"), m).then_inc(bank_free[k], 1)

                for u in range(NG * NU):
                    l = u % NU
                    if u >= 2:
                        if (l - 2) % NU in CHUNK_END:
                            out_chunk(u - 2)
                        act.wait_ge(av_done, u - 1)
                    n(av_done)
                    act.wait_ge(sc_ready, n(sc_ready))
                    w = width(l)
                    s = sc[:, u % 2, :, 0:w]
                    p = probs[:, u % 2, :, 0:w]
                    nc.scalar.activation(p, s, ACT.Exp).then_inc(exp_done, 1)
                    for job in jobs.get(u - 2, []):
                        if job[0] == "T":
                            second_part(job[1])
                    for job in jobs.get(u - 1, []):
                        job_part(job)
                for job in jobs[NG * NU - 1]:
                    job_part(job)
                out_chunk(NG * NU - 1)
                for job in [] if nxt else TAIL:
                    job_part(job)
                n.settle()

            body(0, False, True)
            with act.Fori(1, B - 1) as b:
                body(b, True, True)
            act.wait_ge(lut_done, 1)
            body(B - 1, True, False)

            def ffn_pair(more):
                for c in range(2):
                    for oc in range(OC):
                        act.wait_ge(f_gu_ready, n(f_gu_ready))
                        nc.scalar.activation(silu[:, oc % 2, :], GB[oc % 2], ACT.Silu).then_inc(f_silu_ready, 1)
                    for p in range(TC // 2) if more or c == 0 else []:
                        act.wait_ge(f_tr_ready, n(f_tr_ready))
                        x_high(1 - c, p, TB[p])
                n.settle()

            with act.Fori(0, NCHUNK // 2 - 1) as i:
                ffn_pair(True)
            ffn_pair(False)

        @block.vector
        def _(dve):
            n = Tally(dve)

            def own():
                nc.vector.engine_nop().then_inc(dve_self, 1)
                dve.wait_ge(dve_self, n(dve_self))

            def signal(s):
                nc.vector.engine_nop().then_inc(s, 1)

            banks = Banks()

            nc.vector.memset(ones3[:, :], 1.0)
            nc.vector.memset(mfull[:, :], LEAST)
            for c in [k * OCP for k in range(2 * KD)]:
                nc.vector.memset(idxT[:, c + INTER:c + OCP], -1.0)
            nc.vector.memset(idxT[:, DOWN0 + (OC - 1) * D:], -1.0)
            def rows_var(m):
                own()
                for t in range(m):
                    nc.vector.bn_aggr(mv[:, t, :], stats[:, t, :])
                own()
                nc.vector.tensor_scalar(var[:, 0:m], mv[:, 0:m, 1], 1e-5, None, ALU.add).then_inc(var_ready, 1)

            def normed(to, row, t):
                return nc.vector.tensor_scalar(to, row, mv[:, t, 0:1], rstd[:, t:t + 1], ALU.subtract, ALU.mult)

            def batch_stats(i):
                if i == 0:
                    dve.wait_ge(x_in, n(x_in, 16))
                for t in (2 * i, 2 * i + 1):
                    nc.vector.bn_stats(stats[:, t, :], xin[:, t, :])
                if i == RT // 2 - 1:
                    rows_var(RT)

            def norm_tile(t):
                if t == 0:
                    dve.wait_ge(rstd_ready, n(rstd_ready))
                dve.wait_ge(xn_free, n(xn_free))
                normed(xn[:, t % 2, :], xin[:, t, :], t).then_inc(xn_ready, 1)
                if t == RT - 1:
                    signal(xin_used)

            def qk_norm(t):
                dve.wait_ge(rs_ready, n(rs_ready))
                for i in range(2):
                    last = nc.vector.scalar_tensor_tensor(
                        out=qkn[:, i * D:(i + 1) * D], in0=qkraw[:, t % 2, i * D:(i + 1) * D],
                        scalar=rs[:, t % 2, i:i + 1], in1=lnw[:, i * D:(i + 1) * D], op0=ALU.mult, op1=ALU.mult)
                last.then_inc(qkn_ready, 1)

            def t_part(t):
                dve.wait_ge(rest_free, n(rest_free))
                dve.wait_ge(p1_ready, n(p1_ready))
                k, m = banks.of("T", t)
                nc.vector.tensor_tensor(rest[:, t % 2, :].rearrange("p (a r) -> p a r", a=4),
                                        m.rearrange("p (a r) -> p a r", a=4),
                                        parts[:, 0, :, t * P:(t + 1) * P], ALU.subtract).then_inc(bank_free[k], 1)
                signal(r1_ready)

            def fill_part(group, f):
                k, m = banks.of("fill", group, f)
                dve.wait_ge(fill_ready, n(fill_ready))
                h, pieces = f // len(FILLS), FILLS[f % len(FILLS)]
                for qt, k0, w, col, diag in pieces:
                    src = m[:, col:col + w]
                    at = slice(h * RT + qt, h * RT + qt + 1)
                    if diag:
                        last = nc.vector.tensor_tensor_reduce(
                            out=maxj[:, k, col:col + w], in0=src, in1=causal[:, BANK - w:], scale=1.0, scalar=LEAST,
                            op0=ALU.add, op1=ALU.max, accum_out=mdiag[:, at])
                    else:
                        last = nc.vector.reduce_max(mfull[:, at], src, AX_X)
                last.then_inc(bank_free[k], 1)

            def cut_maxima():
                own()
                nc.vector.tensor_tensor(mrow[:, :], mdiag[:, :], mfull[:, :], ALU.max)
                own()
                nc.vector.tensor_scalar(mrest[:, 0, :], mrow[:, :], -1.0, None, ALU.mult)
                own()
                nc.vector.tensor_copy(mcut[:, 0, :], mrest[:, 0, :])
                own()
                nc.vector.tensor_tensor(mrest[:, 1, :], mrest[:, 0, :], mcut[:, 0, :], ALU.subtract)
                own()
                nc.vector.tensor_copy(mcut[:, 1, :], mrest[:, 1, :])
                own()
                nc.vector.tensor_tensor(mcut[:, 2, :], mrest[:, 1, :], mcut[:, 1, :],
                                        ALU.subtract).then_inc(mcut_ready, 1)

            def n_part(group):
                dve.wait_ge(misc_dve, n(misc_dve))
                k, m = banks.of("N", group)
                nc.vector.tensor_copy(mcutT[0:96, :], m[0:96, 0:P // 2].bitcast(BF16)).then_inc(bank_free[k], 1)
                signal(mcutT_ready)

            dve.sem_inc(xn_free, 2)
            dve.sem_inc(rest_free, 2)
            for i in range(RT // 2):
                batch_stats(i)
            dve.wait_ge(bias_in, 16 * 2)
            nc.vector.tensor_copy(bias_cut[:, 0, :], bias_row[:, :])
            own()
            nc.vector.tensor_tensor(bias_rest[:, :], bias_row[:, :], bias_cut[:, 0, :], ALU.subtract)
            own()
            nc.vector.tensor_copy(bias_cut[:, 1, :], bias_rest[:, :])
            own()
            nc.vector.tensor_tensor(bias_cut[:, 2, :], bias_rest[:, :], bias_cut[:, 1, :],
                                    ALU.subtract).then_inc(bias_cut_ready, 1)
            norm_tile(0)
            norm_tile(1)
            dve.wait_ge(consts_in, 16 * 3)
            nc.vector.tensor_scalar(lnw[:, 0:D], lnw[:, 0:D], float(D ** 0.5) / float(HD ** 0.5), None, ALU.mult)
            nc.vector.tensor_scalar(lnw[:, D:], lnw[:, D:], float(D ** 0.5), None, ALU.mult)
            own()
            for step in STEPS:
                for kind, t in step:
                    if kind == "X" and 0 < t < RT - 1:
                        norm_tile(t + 1)
                        if t <= NG:
                            nc.vector.memset(ks[t - 1][KROWS:SROWS, :, :].rearrange("p h s -> p (h s)").bitcast(F32), TWO_ONES)
                    if kind == "R":
                        qk_norm(t)
                    elif kind == "T":
                        t_part(t)
                    else:
                        banks.of(kind, t)
            n.settle()
            banks.turns = START_TURNS
            for f in range(NF):
                fill_part(0, f)
            cut_maxima()
            n_part(0)
            for f in EARLY:
                fill_part(1, f)
            dve.sem_inc(picked_free, 2)
            for i in range(2):
                dve.sem_inc(x2_stored[i], 16)
            n.settle()

            def chunk_stats(c, tiles):
                if 0 in tiles:
                    dve.wait_ge(f_x2_in[c], n(f_x2_in[c], 16))
                for t in tiles:
                    nc.vector.bn_stats(stats[:, t, :], x2f[:, c, t, :])

            def norm_rows(c):
                dve.wait_ge(rstd_ready, n(rstd_ready))
                for t in range(TC):
                    normed(xnf[t], x2f[:, c, t, :], t).then_inc(f_xn_ready, 1)

            def x_low(c, p, bank):
                dve.wait_ge(f_xhi_ready, n(f_xhi_ready))
                cols = slice(2 * p * P, 2 * (p + 1) * P)
                return nc.vector.tensor_tensor(xTl[:, c, :, cols].rearrange("p k (t r) -> p t k r", t=2),
                                               bank.rearrange("p (t k r) -> p t k r", t=2, k=KD),
                                               xTh[:, c, :, cols].rearrange("p k (t r) -> p t k r", t=2).bitcast(F32),
                                               ALU.subtract)

            def body(b, carry, nxt):
                jobs = place_jobs(carry, nxt)
                banks.turns = BODY_TURNS[carry, nxt]
                step = 0

                def job_part(job):
                    kind = job[0]
                    if kind == "T":
                        t_part(job[1])
                    elif kind == "R":
                        qk_norm(job[1])
                    elif kind == "S":
                        chunk_stats(0, range(TC))
                        rows_var(TC)
                    elif kind == "FN":
                        norm_rows(0)
                    elif kind == "FT":
                        k, m = banks.of(*job)
                        x_low(0, job[1], m).then_inc(bank_free[k], 1)
                    elif kind == "W":
                        dve.wait_ge(f_w_hi, n(f_w_hi))
                        cols = slice(job[1] * BANK, (job[1] + 1) * BANK)
                        nc.vector.tensor_tensor(wlo[:, cols], wlook[:, cols], whi[:, cols].bitcast(F32), ALU.subtract)
                    elif kind == "N":
                        n_part(job[1])
                    elif kind == "C":
                        g, qc = job[1:3]
                        dve.wait_ge(misc_dve, n(misc_dve))
                        k, m = banks.of(*job)
                        o = m[:, 0:2 * P].rearrange("p (t h c) -> p t h c", t=2, h=GH)
                        nc.vector.reciprocal(rden[:, qc % 2, :, :], o[:, :, :, HD])
                        own()
                        nc.vector.tensor_tensor(
                            attn[:, 2 * qc:2 * qc + 2, g * GH * HD:(g + 1) * GH * HD].rearrange("p t (h c) -> p t h c", h=GH),
                            o[:, :, :, 0:HD], rden[:, qc % 2, :, :].unsqueeze(3).broadcast_to([P, 2, GH, HD]),
                            ALU.mult).then_inc(bank_free[k], 1)
                    elif kind == "OP":
                        t = job[1]
                        dve.wait_ge(x2_stored[t % 2], n(x2_stored[t % 2], 16))
                        dve.wait_ge(xres_in[t % 2], n(xres_in[t % 2], 16))
                        dve.wait_ge(misc_dve, n(misc_dve))
                        k, m = banks.of(*job)
                        nc.vector.tensor_tensor(x2t[:, t % 2, :], m[:, 0:D], xres[:, t % 2, :],
                                                ALU.add).then_inc(bank_free[k], 1)
                        signal(x2_ready)

                for u in range(NG * NU):
                    g, l = divmod(u, NU)
                    for job in jobs[u - 1] if u else []:
                        job_part(job)
                    for group, f in fills_of(u, nxt):
                        fill_part(group, f)
                    if l == CUT_UNIT and (nxt or g < NG - 1):
                        cut_maxima()
                    if nxt and u in STATS_UNITS:
                        batch_stats(STATS_UNITS.index(u))
                    soon = STATS_UNITS[-1] + 1
                    for job in [job for v in range(NG * NU) if max(v - 2, soon) == u for job in jobs[v]]:
                        if job[0] == "X":
                            norm_tile(job[1])
                    if nxt and l in LUT_UNITS:
                        i, j = step % LUTB, step // LUTB
                        dve.wait_ge(picked_free, n(picked_free))
                        nc.vector.tensor_scalar(picked[:, step % 2, :], idxT[:, bass.ds((b * LUTB + i) * BANK, BANK)],
                                                float(j), lut_sb[:, j:j + 1], ALU.is_equal,
                                                ALU.mult).then_inc(picked_ready, 1)
                        step += 1
                for job in jobs[NG * NU - 1] + ([] if nxt else TAIL):
                    job_part(job)
                n.settle()

            body(0, False, True)
            with dve.Fori(1, B - 1) as b:
                body(b, True, True)
            body(B - 1, True, False)

            for i in range(2):
                dve.wait_ge(x2_stored[i], n(x2_stored[i], 16))
                dve.sem_inc(f_stored[i], 16)
            n.settle()

            def ffn_pair(more):
                for c in range(2):
                    ahead = more or c == 0
                    for oc in range(OC):
                        if ahead and oc in STATS_AT:
                            chunk_stats(1 - c, STATS_AT[oc])
                        if ahead and oc == OC - 1:
                            rows_var(TC)
                        dve.wait_ge(f_silu_ready, n(f_silu_ready))
                        nc.vector.tensor_tensor(hf[:, oc % 2, :], silu[:, oc % 2, :], UB[oc % 2], ALU.mult)
                        nc.vector.tensor_tensor(hhi[:, oc, :], silu[:, oc % 2, :], UB[oc % 2],
                                                ALU.mult).then_inc(f_gu_free, 1)
                        own()
                        nc.vector.tensor_tensor(hlo[:, oc, :], hf[:, oc % 2, :], hhi[:, oc, :].bitcast(F32),
                                                ALU.subtract).then_inc(f_h_ready, 1)
                    if ahead:
                        norm_rows(1 - c)
                    for t in range(TC):
                        if ahead and t == 2:
                            for p in range(TC // 2):
                                x_low(1 - c, p, TB[p]).then_inc(f_xT_ready, 1)
                        dve.wait_ge(f_stored[t % 2], n(f_stored[t % 2], 16))
                        dve.wait_ge(f_y_ready, n(f_y_ready))
                        nc.vector.tensor_tensor(yt[:, t % 2, :], YB[t % 2][:, 0:D], x2f[:, c, t, :],
                                                ALU.add).then_inc(f_y_free, 1)
                        signal(f_out_ready)
                    if more:
                        signal(f_x2_used)
                n.settle()

            with dve.Fori(0, NCHUNK // 2 - 1) as i:
                ffn_pair(True)
            ffn_pair(False)
            for i in range(2):
                dve.wait_ge(f_stored[i], n(f_stored[i], 16))

        @block.tensor
        def _(pe):
            n = Tally(pe)

            banks, reads = Banks(), {}

            def take(*use):
                k, m = banks.of(*use)
                pe.wait_ge(bank_free[k], n(bank_free[k]))
                reads[use] = k, n.count(bank_free[k]) + 1
                return m

            def evacuated(*use):
                k, count = reads[use]
                pe.wait_ge(bank_free[k], count)

            def transpose_rows(t):
                m = take("X", t)
                pe.wait_ge(xn_ready, n(xn_ready))
                for h in range(KD):
                    last = nc.tensor.transpose(m[:, h * P:(h + 1) * P], xn[:, t % 2, h * P:(h + 1) * P], ident[:, :])
                last.then_inc(misc_act, 1)

            def project(kind, t):
                m = take(kind, t)
                c0 = "QKV".index(kind) * D
                nc.tensor.matmul(m[:, 0:D], ones3[:, :], bias[:, c0:c0 + D], start=True, stop=False)
                for h in range(KD):
                    last = nc.tensor.matmul(m[:, 0:D], xnT[:, h, t * P:(t + 1) * P], wqkv[:, h, c0:c0 + D],
                                            start=False, stop=h == KD - 1)
                    if kind == "Q" and h == 0:
                        last.then_inc(xn_free, 1)
                last.then_inc(misc_act, 1)

            def queries(t):
                evacuated("X", t)
                project("Q", t)

            def transpose_qk(t):
                m = take("T", t)
                pe.wait_ge(qkn_ready, n(qkn_ready))
                for a in range(4):
                    last = nc.tensor.transpose(m[:, a * P:(a + 1) * P], qkn[:, a * P:(a + 1) * P], ident[:, :])
                last.then_inc(misc_act, 1)

            def fill(group, f):
                m = take("fill", group, f)
                g = group % NG
                h, pieces = f // len(FILLS), FILLS[f % len(FILLS)]
                for qt, k0, w, col, _ in pieces:
                    last = nc.tensor.matmul(m[:, col:col + w], qs[g][0:KROWS, h, qt * P:(qt + 1) * P],
                                            ks[g][0:KROWS, h, k0:k0 + w], start=True, stop=True)
                last.then_inc(fill_ready, 1)

            def transpose_maxima(group):
                m = take("N", group)
                pe.wait_ge(mcut_ready, n(mcut_ready))
                nc.tensor.transpose(m[0:96, 0:P // 2].bitcast(BF16), mcut[:, :, :].rearrange("p a c -> p (a c)"),
                                    identb[:, :]).then_inc(misc_dve, 1)

            def scores(g, l, u):
                qc, kt = UNITS[l]
                w = width(l)
                q0 = (qc + 1) * QC - w
                if l == 0:
                    pe.wait_ge(shift_ready, n(shift_ready, 48))
                for h in range(GH):
                    last = nc.tensor.matmul(sc[:, u % 2, h, 0:w], ks[g][0:SROWS, h, kt * P:(kt + 1) * P],
                                            qs[g][0:SROWS, h, q0:q0 + w], start=True, stop=True)
                last.then_inc(sc_ready, 1)

            for k in range(4):
                pe.sem_inc(bank_free[k], 1)

            pe.wait_ge(made, 1)
            for step in STEPS:
                for kind, t in step:
                    if kind == "X":
                        transpose_rows(t)
                    elif kind == "Q":
                        if t == 0:
                            pe.wait_ge(weights_in, 16)
                            pe.wait_ge(bias_placed, 48)
                        queries(t)
                    elif kind == "K":
                        project("K", t)
                    elif kind == "T":
                        transpose_qk(t)
            for job in (("Q", RT - 1), ("K", RT - 1), ("T", RT - 2), ("T", RT - 1)):
                evacuated(*job)
            n.settle()
            pe.wait_ge(wout_in, 16)
            pe.wait_ge(idx_cast, 1)
            pe.sem_inc(idx_read, 1)
            for seq, (rows, _, _, blocks) in enumerate(IDX_BANKS):
                if seq >= 4:
                    pe.wait_ge(idx_bank_free, seq - 3)
                m, col = PROLOGUE[seq % 4].bitcast(BF16), 0
                for block in blocks:
                    last = nc.tensor.transpose(m[0:rows, col:col + block.shape[0]], block,
                                               identb[0:block.shape[0], 0:block.shape[0]])
                    col += block.shape[0]
                last.then_inc(idx_bank, 1)
            pe.wait_ge(idx_bank_free, len(IDX_BANKS))
            pe.wait_ge(stack_ready[0], n(stack_ready[0], 2 * NTERM * 16))
            banks.turns = START_TURNS
            for f in range(NF):
                fill(0, f)
            transpose_maxima(0)
            for t in range(EARLY_V):
                project("V", t)
            pe.wait_ge(stack_ready[1], n(stack_ready[1], 2 * NTERM * 16))
            for f in EARLY:
                fill(1, f)
                if f == 4:
                    scores(0, 0, 0)
                    scores(0, 1, 1)
            evacuated("V", EARLY_V - 1)
            n.settle()

            def transpose_pair(p, bank, done):
                for i in range(2):
                    pe.wait_ge(f_xn_ready, n(f_xn_ready))
                    for k in range(KD):
                        last = nc.tensor.transpose(bank[:, (i * KD + k) * P:(i * KD + k + 1) * P],
                                                   xnf[2 * p + i][:, k * P:(k + 1) * P], ident[:, :])
                last.then_inc(done, 1)

            def body(b, carry, nxt):
                jobs = place_jobs(carry, nxt)
                banks.turns = BODY_TURNS[carry, nxt]
                total = NG * NU

                def job_part(job):
                    kind = job[0]
                    if kind == "V":
                        project("V", job[1])
                    elif kind == "X":
                        transpose_rows(job[1])
                    elif kind == "Q":
                        queries(job[1])
                    elif kind == "K":
                        project("K", job[1])
                    elif kind == "T":
                        if job[1] == 0:
                            pe.wait_ge(stack_ready[NG - 1], n(stack_ready[NG - 1], 2 * NTERM * 16))
                        transpose_qk(job[1])
                    elif kind == "N":
                        transpose_maxima(job[1])
                    elif kind == "FT":
                        transpose_pair(job[1], take(*job), misc_act)
                    elif kind == "C":
                        g, qc = job[1:3]
                        m = take(*job)
                        if (g, qc) == (NG - 1, NQC - 1):
                            pe.wait_ge(oT_ready, n(oT_ready))
                        for i in range(2):
                            last = nc.tensor.transpose(m[:, i * P:(i + 1) * P],
                                                       oT[:, (g * NQC + qc) % 2, i * P:(i + 1) * P], ident[:, :])
                        last.then_inc(misc_dve, 1)
                    elif kind == "OT":
                        evacuated("C", NG - 1, *job[1:])
                        m = take(*job)
                        for i in range(2):
                            for k in range(KD):
                                last = nc.tensor.transpose(m[:, (i * KD + k) * P:(i * KD + k + 1) * P],
                                                           attn[:, 2 * job[1] + i, k * P:(k + 1) * P], ident[:, :])
                        last.then_inc(misc_act, 1)
                    elif kind == "OP":
                        evacuated("OT", job[1] // 2, *job[2:])
                        m = take(*job)
                        nc.tensor.matmul(m[:, 0:D], ones3[:, :], bias[:, 3 * D:], start=True, stop=False)
                        for k in range(KD):
                            last = nc.tensor.matmul(m[:, 0:D], attnT[:, job[1] % 2, k, :], wout[:, k, :],
                                                    start=False, stop=k == KD - 1)
                        last.then_inc(misc_dve, 1)

                for u in range(total):
                    g, l = divmod(u, NU)
                    fills = fills_of(u, nxt)

                    def some_fills(k):
                        for _ in range(min(k, len(fills))):
                            group, f = fills.pop(0)
                            if f == 0 and group != NG - 1 or (group, f) == (NG - 1, 0) and not nxt:
                                pe.wait_ge(stack_ready[group % NG], n(stack_ready[group % NG], 2 * NTERM * 16))
                            fill(group, f)

                    some_fills(1)
                    pe.wait_ge(exp_done, n(exp_done))
                    if is_diag(l):
                        pe.sem_inc(exp_diag, 1)
                    if u + 2 < total:
                        scores((u + 2) // NU, (u + 2) % NU, u + 2)
                    elif nxt:
                        scores(0, (u + 2) % NU, u + 2)
                    for job in jobs[u]:
                        job_part(job)
                    some_fills(1)
                    if g == 0 and is_diag(l) and UNITS[l][1] >= EARLY_V:
                        evacuated("V", UNITS[l][1])
                    if is_diag(l):
                        pe.wait_ge(masked, n(masked))
                    qc, kt = UNITS[l]
                    if kt == 0 and u > 0:
                        pe.wait_ge(oT_ready, n(oT_ready))
                    w = width(l)
                    for h in range(GH):
                        last = nc.tensor.matmul(ov[32 * h:32 * (h + 1), QC - w:QC],
                                                vaug[:, kt, g * GH + h, :], probs[:, u % 2, h, 0:w],
                                                start=kt == 0, stop=kt == 2 * qc + 1)
                        if h == 0 and l == NU - 3:
                            last.then_inc(stack_free, 1)
                    last.then_inc(av_done, 1)
                    some_fills(len(fills))
                for job in [] if nxt else TAIL:
                    job_part(job)
                if nxt:
                    evacuated("V", EARLY_V - 1)
                n.settle()

            body(0, False, True)
            with pe.Fori(1, B - 1) as b:
                body(b, True, True)
            body(B - 1, True, False)

            for k in range(NRING):
                pe.wait_ge(bank_free[k], 1)

            pe.sem_inc(f_gu_free, 2)
            pe.sem_inc(f_y_free, 2)
            n.settle()

            def weight(at, width, high):
                return (whi if high else wlo)[:, at:at + width]

            def ffn_pair(more):
                for c in range(2):
                    ahead = more or c == 0
                    for oc in range(OC):
                        pe.wait_ge(f_gu_free, n(f_gu_free))
                        for col0, dst in ((0, GB[oc % 2]), (UP0, UB[oc % 2])):
                            terms = [(k, wh, xh) for k in range(KD) for wh, xh in ((1, 1), (0, 1), (1, 0))]
                            for i, (k, wh, xh) in enumerate(terms):
                                last = nc.tensor.matmul(dst, weight(col0 + k * OCP + oc * P, P, wh), (xTh if xh else xTl)[:, c, k, :],
                                                        start=i == 0, stop=i == len(terms) - 1)
                        last.then_inc(f_gu_ready, 1)
                    for p in range(TC // 2):
                        if ahead and p == 1:
                            for i in range(TC // 2):
                                transpose_pair(i, TB[i], f_tr_ready)
                        for pieces in (range(OC - 1), range(OC - 1, OC)):
                            for i in range(2):
                                t = 2 * p + i
                                if 0 in pieces:
                                    pe.wait_ge(f_y_free, n(f_y_free))
                                for oc in pieces:
                                    if t == 0:
                                        pe.wait_ge(f_h_ready, n(f_h_ready))
                                    for j, (hh, wh) in enumerate(((1, 1), (0, 1), (1, 0))):
                                        last = nc.tensor.matmul(YB[i][:, 0:D], (hhi if hh else hlo)[:, oc, t * P:(t + 1) * P],
                                                                weight(DOWN0 + oc * D, D, wh), start=oc == 0 and j == 0,
                                                                stop=oc == OC - 1 and j == 2)
                                if OC - 1 in pieces:
                                    last.then_inc(f_y_ready, 1)
                    if ahead:
                        pe.wait_ge(f_xT_ready, n(f_xT_ready, 2))
                n.settle()

            with pe.Fori(0, NCHUNK // 2 - 1) as i:
                ffn_pair(True)
            ffn_pair(False)


_INS = ['L0_attn_x', 'L0_attn_w_qkv', 'L0_attn_b_qkv', 'L0_attn_q_ln_w', 'L0_attn_k_ln_w', 'L0_attn_w_out',
        'L0_attn_b_out', 'L0_ffn_lut', 'L0_ffn_gate_idx', 'L0_ffn_up_idx', 'L0_ffn_down_idx']


def kernel(**inputs):
    import numpy as _np
    import concourse.bacc as _bacc
    from concourse import mybir as _mybir
    from concourse.bass_utils import run_bass_kernel_spmd as _run

    nc = _bacc.Bacc("TRN2", target_bir_lowering=False, num_devices=1)
    arrays, args = {}, []
    for name in _INS:
        a = _np.ascontiguousarray(inputs[name])
        arrays[f"in_{name}_dram"] = a
        args.append(nc.dram_tensor(f"in_{name}_dram", a.shape, _mybir.dt.from_np(a.dtype), kind="ExternalInput").ap())
    shape = inputs['L0_attn_x'].shape
    args.append(nc.dram_tensor("out_0_dram", shape, _mybir.dt.float32, kind="ExternalOutput").ap())
    layer_kernel(nc, *args)
    r = _run(nc, [arrays], core_ids=[0])
    return r.results[0]["out_0_dram"]
```
